# Optimizing a Trainium2 kernel written in Bass

```python
import numpy as np
import jax
import jax.numpy as jnp

def _softmax(x, axis=-1):
    return jax.nn.softmax(x, axis=axis)

def _gelu(x):
    return jax.nn.gelu(x, approximate=True)

def _silu(x):
    return jax.nn.silu(x)

def _sigmoid(x):
    return jax.nn.sigmoid(x)

def _layernorm(x, axis=-1, eps=1e-05):
    m = jnp.mean(x, axis=axis, keepdims=True)
    v = jnp.var(x, axis=axis, keepdims=True)
    return (x - m) / jnp.sqrt(v + eps)

def _scatter_add(tgt, idx, src, axis=0):
    return tgt.at[idx].add(src)

def _segment_sum(src, seg, n):
    return jax.ops.segment_sum(src, seg, n)
kernel_name = 'mk_flamingo_gated_d4_seqx_r8_7a48c4'

def setup_inputs(seed: int=0):
    np.random.seed(seed)
    _w = jnp.asarray

    def _rec_inputs():
        import jax
        import jax.numpy as jnp
        _rk = jax.random.key(seed)
        x = -0.0003929 + 0.9999 * jax.random.normal(jax.random.fold_in(_rk, 1), (8, 128, 128), jnp.float32)
        _lenS = 128 - jax.random.randint(jax.random.fold_in(_rk, 7), (8,), 0, max(1, 128 // 4) + 1, jnp.int32)
        _lenS2 = 77 - jax.random.randint(jax.random.fold_in(_rk, 8), (8,), 0, max(1, 77 // 4) + 1, jnp.int32)
        _ctx_1024P = jax.random.normal(jax.random.fold_in(_rk, 11), (8, 16, 128), jnp.float32)
        _ctx_1024c = jax.random.dirichlet(jax.random.fold_in(_rk, 511), 0.3 * jnp.ones((16,), jnp.float32), (8, 77))
        _ctx_1024t = jnp.einsum('bsk,bkd->bsd', _ctx_1024c, _ctx_1024P)
        _ctx_1024t = _ctx_1024t * jax.lax.rsqrt(jnp.mean(jnp.square(_ctx_1024t)) + 1e-12) * 0.953939
        ctx_1024 = 2.81802e-05 + 1.00001 * (_ctx_1024t + 0.3 * jax.random.normal(jax.random.fold_in(_rk, 611), (8, 77, 128), jnp.float32))
        _validS = jnp.arange(128)[None, :] < _lenS[:, None]
        _validS2 = jnp.arange(77)[None, :] < _lenS2[:, None]
        _causal = jnp.tril(jnp.ones((128, 128), dtype=bool))
        mask_Bx1xS2_ik0 = jnp.where(jnp.broadcast_to(_validS2[:, None, :], (8, 1, 77)), 0, 1).astype(jnp.int32)
        mask_Bx1xSxS2_ik1 = jnp.where(jnp.broadcast_to(_validS2[:, None, None, :], (8, 1, 128, 77)), 1, 0).astype(jnp.int32)
        _g = jax.random.normal(jax.random.fold_in(_rk, 9001), (2, 4), jnp.float32)
        _g = jnp.sign(_g) * jnp.maximum(jnp.abs(_g), 1.0) + (_g == 0) * 1.0
        g_xattn = _g[0]
        g_ffn = _g[1]
        return (x, ctx_1024, mask_Bx1xS2_ik0, mask_Bx1xSxS2_ik1, g_xattn, g_ffn)
    x, ctx_1024, mask_Bx1xS2_ik0, mask_Bx1xSxS2_ik1, g_xattn, g_ffn = _rec_inputs()

    def _L0_xattn_setup():
        import jax, jax.numpy as jnp
        import numpy as np
        B, N, D, R = (4, 512, 128, 32)
        key = jax.random.key(seed)
        k1, k2, k3, k4, k5 = jax.random.split(key, 5)
        q = jax.random.normal(k1, (B, N, D), dtype=jnp.float32)
        k = jax.random.normal(k2, (B, N, D), dtype=jnp.float32)
        v = jax.random.normal(k3, (B, N, D), dtype=jnp.float32)
        Wu = jax.random.normal(k4, (D, R), dtype=jnp.float32) * (1.0 / np.sqrt(D))
        Wv = jax.random.normal(k5, (D, R), dtype=jnp.float32) * (1.0 / np.sqrt(D))
        return {'q': q, 'k': k, 'v': v, 'Wu': Wu, 'Wv': Wv}
    _L0_xattn_all = _L0_xattn_setup()
    _L0_xattn_in = {k: v for k, v in _L0_xattn_all.items() if k in ('Wu', 'Wv')}
    del _L0_xattn_all

    def _L0_ffn_setup():
        import jax, jax.numpy as jnp
        import numpy as np
        HIDDEN = 128
        N_EXPERTS = 8
        TOP_K = 2
        INTER = 176
        N_SHARED = 2
        SCALE = 1.0
        key = jax.random.key(seed)
        ks = jax.random.split(key, 9)
        s_h = 1.0 / np.sqrt(HIDDEN)
        s_i = 1.0 / np.sqrt(INTER)
        x = jax.random.normal(ks[0], (2, 256, HIDDEN), dtype=jnp.float32)
        gate_w = jax.random.uniform(ks[1], (N_EXPERTS, HIDDEN), jnp.float32, -s_h, s_h)
        wg = jax.random.uniform(ks[2], (N_EXPERTS, HIDDEN, INTER), jnp.float32, -s_h, s_h)
        wu = jax.random.uniform(ks[3], (N_EXPERTS, HIDDEN, INTER), jnp.float32, -s_h, s_h)
        wd = jax.random.uniform(ks[4], (N_EXPERTS, INTER, HIDDEN), jnp.float32, -s_i, s_i)
        si = INTER * N_SHARED
        s_si = 1.0 / np.sqrt(si)
        swg = jax.random.uniform(ks[5], (HIDDEN, si), jnp.float32, -s_h, s_h)
        swu = jax.random.uniform(ks[6], (HIDDEN, si), jnp.float32, -s_h, s_h)
        swd = jax.random.uniform(ks[7], (si, HIDDEN), jnp.float32, -s_si, s_si)
        return {'x': x, 'gate_w': gate_w, 'wg': wg, 'wu': wu, 'wd': wd, 'swg': swg, 'swu': swu, 'swd': swd}
    _L0_ffn_all = _L0_ffn_setup()
    _L0_ffn_in = {k: v for k, v in _L0_ffn_all.items() if k in ('gate_w', 'wg', 'wu', 'wd', 'swg', 'swu', 'swd')}
    del _L0_ffn_all

    def _L1_xattn_setup():
        import jax, jax.numpy as jnp
        import numpy as np
        import math
        N_HEAD = 16
        N_FEAT = 128
        D_K = N_FEAT // N_HEAD
        key = jax.random.key(seed)
        k1, k2, k3, k4, k5, k6 = jax.random.split(key, 6)
        B, T1, T2 = (4, 256, 256)
        query = jax.random.normal(k1, (B, T1, N_FEAT), dtype=jnp.float32)
        key_t = jax.random.normal(k2, (B, T2, N_FEAT), dtype=jnp.float32)
        value = jax.random.normal(k3, (B, T2, N_FEAT), dtype=jnp.float32)
        mask = jax.random.randint(k4, (B, 1, T2), 0, 2, dtype=jnp.int32)
        bound = 1.0 / math.sqrt(N_FEAT)
        Wq = jax.random.uniform(k5, (N_FEAT, N_FEAT), minval=-bound, maxval=bound, dtype=jnp.float32)
        bq = jax.random.uniform(k6, (N_FEAT,), minval=-bound, maxval=bound, dtype=jnp.float32)
        return {'query': query, 'key': key_t, 'value': value, 'mask': mask, 'Wq': Wq, 'bq': bq}
    _L1_xattn_all = _L1_xattn_setup()
    _L1_xattn_in = {k: v for k, v in _L1_xattn_all.items() if k in ('Wq', 'bq')}
    del _L1_xattn_all

    def _L1_ffn_setup():
        import jax, jax.numpy as jnp
        import numpy as np
        B, S, H, F, E, K = (2, 256, 128, 512, 8, 2)

        def _ln(x, g, b, eps=1e-05):
            m = jnp.mean(x, axis=-1, keepdims=True)
            v = jnp.var(x, axis=-1, keepdims=True)
            return (x - m) / jnp.sqrt(v + eps) * g + b

        def _gelu(x):
            return jax.nn.gelu(x, approximate=False)
        key = jax.random.key(seed)
        ks = jax.random.split(key, 12)
        F2 = F // 2
        return {'hidden_states': jax.random.normal(ks[0], (B, S, H), jnp.float32), 'ln_g': jnp.ones((H,), jnp.float32), 'ln_b': jnp.zeros((H,), jnp.float32), 'router_w': jax.random.normal(ks[1], (H, E), jnp.float32) * 0.01, 'up_W': jax.random.normal(ks[2], (E, H, F), jnp.float32) * 0.02, 'up_b': jnp.zeros((E, F), jnp.float32), 'down_W': jax.random.normal(ks[3], (E, F, H), jnp.float32) * 0.02, 'down_b': jnp.zeros((E, H), jnp.float32), 'spec0_W': jax.random.normal(ks[4], (2, F, F), jnp.float32) * 0.02, 'spec0_b': jnp.zeros((2, F), jnp.float32), 'ln0_g': jnp.ones((2, F), jnp.float32), 'ln0_b': jnp.zeros((2, F), jnp.float32), 'spec1a_W': jax.random.normal(ks[5], (2, F, F2), jnp.float32) * 0.02, 'spec1a_b': jnp.zeros((2, F2), jnp.float32), 'spec1b_W': jax.random.normal(ks[6], (2, F2, F), jnp.float32) * 0.02, 'spec1b_b': jnp.zeros((2, F), jnp.float32), 'ln1_g': jnp.ones((2, F), jnp.float32), 'ln1_b': jnp.zeros((2, F), jnp.float32), 'spec2_W': jax.random.normal(ks[7], (2, F, F), jnp.float32) * 0.02, 'spec2_b': jnp.zeros((2, F), jnp.float32)}
    _L1_ffn_all = _L1_ffn_setup()
    _L1_ffn_in = {k: v for k, v in _L1_ffn_all.items() if k in ('ln_g', 'ln_b', 'router_w', 'up_W', 'up_b', 'down_W', 'down_b', 'spec0_W', 'spec0_b', 'ln0_g', 'ln0_b', 'spec1a_W', 'spec1a_b', 'spec1b_W', 'spec1b_b', 'ln1_g', 'ln1_b', 'spec2_W', 'spec2_b')}
    del _L1_ffn_all

    def _L2_xattn_setup():
        import jax, jax.numpy as jnp
        import numpy as np
        D1, D2, D3 = (128, 128, 128)
        key = jax.random.key(seed)
        k1, k2, kw, kb = jax.random.split(key, 4)
        x1 = jax.random.normal(k1, (8, 256, D1), dtype=jnp.float32)
        x2 = jax.random.normal(k2, (8, 256, D2), dtype=jnp.float32)
        bound = 1.0 / np.sqrt(D1 + D2)
        W = jax.random.uniform(kw, (D3, D1 + D2), minval=-bound, maxval=bound, dtype=jnp.float32)
        b = jax.random.uniform(kb, (D3,), minval=-bound, maxval=bound, dtype=jnp.float32)
        return {'x1': x1, 'x2': x2, 'W': W, 'b': b}
    _L2_xattn_all = _L2_xattn_setup()
    _L2_xattn_in = {k: v for k, v in _L2_xattn_all.items() if k in ('W', 'b')}
    del _L2_xattn_all

    def _L2_ffn_setup():
        import jax, jax.numpy as jnp
        import numpy as np
        BLOCK = 16
        _GRID = jnp.array([0.0, 0.5, 1.0, 1.5, 2.0, 3.0, 4.0, 6.0], dtype=jnp.float32)
        _MID = jnp.array([0.25, 0.75, 1.25, 1.75, 2.5, 3.5, 5.0], dtype=jnp.float32)

        def fp4_quant_dequant(x):
            shape = x.shape
            xb = x.reshape(shape[:-1] + (shape[-1] // BLOCK, BLOCK))
            scale = jnp.max(jnp.abs(xb), axis=-1, keepdims=True) / 6.0
            scale = jnp.maximum(scale, jnp.float32(1e-12))
            xn = xb / scale
            idx = jnp.searchsorted(_MID, jnp.abs(xn))
            q = _GRID[idx] * jnp.sign(xn) * scale
            return q.reshape(shape)

        def fp4_linear(x, w):
            xq = fp4_quant_dequant(x)
            wq = fp4_quant_dequant(w)
            return jnp.einsum('bsk,nk->bsn', xq, wq)
        key = jax.random.key(seed)
        k1, k2, k3, k4 = jax.random.split(key, 4)
        H, I = (128, 352)
        x = jax.random.normal(k1, (4, 512, H), dtype=jnp.float32)
        w_gate = jax.random.normal(k2, (I, H), dtype=jnp.float32) * 0.02
        w_up = jax.random.normal(k3, (I, H), dtype=jnp.float32) * 0.02
        w_down = jax.random.normal(k4, (H, I), dtype=jnp.float32) * 0.02
        return {'x': x, 'w_gate': w_gate, 'w_up': w_up, 'w_down': w_down}
    _L2_ffn_all = _L2_ffn_setup()
    _L2_ffn_in = {k: v for k, v in _L2_ffn_all.items() if k in ('w_gate', 'w_up', 'w_down')}
    del _L2_ffn_all

    def _L3_xattn_setup():
        import jax, jax.numpy as jnp
        import numpy as np
        EMBED_SIZE = 128
        HEADS = 16
        HEAD_DIM = EMBED_SIZE // HEADS
        key = jax.random.key(seed)
        ks = jax.random.split(key, 9)
        N, S = (4, 256)
        query = jax.random.normal(ks[0], (N, S, EMBED_SIZE), dtype=jnp.float32)
        keys = jax.random.normal(ks[1], (N, S, EMBED_SIZE), dtype=jnp.float32)
        values = jax.random.normal(ks[2], (N, S, EMBED_SIZE), dtype=jnp.float32)
        mask = jax.random.randint(ks[3], (N, 1, S, S), 0, 2, dtype=jnp.int32)
        sc = 1.0 / np.sqrt(HEAD_DIM)
        Wq = jax.random.normal(ks[4], (HEAD_DIM, HEAD_DIM), dtype=jnp.float32) * sc
        Wk = jax.random.normal(ks[5], (HEAD_DIM, HEAD_DIM), dtype=jnp.float32) * sc
        Wv = jax.random.normal(ks[6], (HEAD_DIM, HEAD_DIM), dtype=jnp.float32) * sc
        Wo = jax.random.normal(ks[7], (EMBED_SIZE, EMBED_SIZE), dtype=jnp.float32) / np.sqrt(EMBED_SIZE)
        bo = jax.random.normal(ks[8], (EMBED_SIZE,), dtype=jnp.float32) * 0.01
        return {'query': query, 'keys': keys, 'values': values, 'mask': mask, 'Wq': Wq, 'Wk': Wk, 'Wv': Wv, 'Wo': Wo, 'bo': bo}
    _L3_xattn_all = _L3_xattn_setup()
    _L3_xattn_in = {k: v for k, v in _L3_xattn_all.items() if k in ('Wq', 'Wk', 'Wv', 'Wo', 'bo')}
    del _L3_xattn_all

    def _L3_ffn_setup():
        import jax, jax.numpy as jnp
        import numpy as np
        NEG_INF = -1e+30

        def _moe_forward(x, router_w, router_b, w1, b1, w2, b2, top_k=2):
            B, S, D = x.shape
            E = router_w.shape[1]
            logits = jnp.einsum('bsd,de->bse', x, router_w) + router_b
            top_vals, top_idx = jax.lax.top_k(logits, top_k)
            keep = jax.nn.one_hot(top_idx, E, dtype=logits.dtype).sum(-2) > 0
            sparse_logits = jnp.where(keep, logits, NEG_INF)
            gating = jax.nn.softmax(sparse_logits, axis=-1)
            xf = x.reshape(-1, D)
            gf = gating.reshape(-1, E)
            h = jax.nn.relu(jnp.einsum('td,edh->eth', xf, w1) + b1[:, None, :])
            y = jnp.einsum('eth,ehd->etd', h, w2) + b2[:, None, :]
            out = jnp.einsum('etd,te->td', y, gf)
            return out.reshape(B, S, D)
        key = jax.random.key(seed)
        ks = jax.random.split(key, 5)
        B, S, D, E, H = (2, 256, 128, 8, 512)
        scale = 0.02
        return {'x': jax.random.normal(ks[0], (B, S, D), dtype=jnp.float32), 'router_w': jax.random.normal(ks[1], (D, E), dtype=jnp.float32) * scale, 'router_b': jnp.zeros((E,), dtype=jnp.float32), 'w1': jax.random.normal(ks[2], (E, D, H), dtype=jnp.float32) * scale, 'b1': jnp.zeros((E, H), dtype=jnp.float32), 'w2': jax.random.normal(ks[3], (E, H, D), dtype=jnp.float32) * scale, 'b2': jnp.zeros((E, D), dtype=jnp.float32)}
    _L3_ffn_all = _L3_ffn_setup()
    _L3_ffn_in = {k: v for k, v in _L3_ffn_all.items() if k in ('router_w', 'router_b', 'w1', 'b1', 'w2', 'b2')}
    del _L3_ffn_all
    return {'x': x, 'ctx_1024': ctx_1024, 'mask_Bx1xS2_ik0': mask_Bx1xS2_ik0, 'mask_Bx1xSxS2_ik1': mask_Bx1xSxS2_ik1, 'g_xattn': g_xattn, 'g_ffn': g_ffn, 'L0_xattn_Wu': _L0_xattn_in['Wu'], 'L0_xattn_Wv': _L0_xattn_in['Wv'], 'L0_ffn_gate_w': _L0_ffn_in['gate_w'], 'L0_ffn_wg': _L0_ffn_in['wg'], 'L0_ffn_wu': _L0_ffn_in['wu'], 'L0_ffn_wd': _L0_ffn_in['wd'], 'L0_ffn_swg': _L0_ffn_in['swg'], 'L0_ffn_swu': _L0_ffn_in['swu'], 'L0_ffn_swd': _L0_ffn_in['swd'], 'L1_xattn_Wq': _L1_xattn_in['Wq'], 'L1_xattn_bq': _L1_xattn_in['bq'], 'L1_ffn_ln_g': _L1_ffn_in['ln_g'], 'L1_ffn_ln_b': _L1_ffn_in['ln_b'], 'L1_ffn_router_w': _L1_ffn_in['router_w'], 'L1_ffn_up_W': _L1_ffn_in['up_W'], 'L1_ffn_up_b': _L1_ffn_in['up_b'], 'L1_ffn_down_W': _L1_ffn_in['down_W'], 'L1_ffn_down_b': _L1_ffn_in['down_b'], 'L1_ffn_spec0_W': _L1_ffn_in['spec0_W'], 'L1_ffn_spec0_b': _L1_ffn_in['spec0_b'], 'L1_ffn_ln0_g': _L1_ffn_in['ln0_g'], 'L1_ffn_ln0_b': _L1_ffn_in['ln0_b'], 'L1_ffn_spec1a_W': _L1_ffn_in['spec1a_W'], 'L1_ffn_spec1a_b': _L1_ffn_in['spec1a_b'], 'L1_ffn_spec1b_W': _L1_ffn_in['spec1b_W'], 'L1_ffn_spec1b_b': _L1_ffn_in['spec1b_b'], 'L1_ffn_ln1_g': _L1_ffn_in['ln1_g'], 'L1_ffn_ln1_b': _L1_ffn_in['ln1_b'], 'L1_ffn_spec2_W': _L1_ffn_in['spec2_W'], 'L1_ffn_spec2_b': _L1_ffn_in['spec2_b'], 'L2_xattn_W': _L2_xattn_in['W'], 'L2_xattn_b': _L2_xattn_in['b'], 'L2_ffn_w_gate': _L2_ffn_in['w_gate'], 'L2_ffn_w_up': _L2_ffn_in['w_up'], 'L2_ffn_w_down': _L2_ffn_in['w_down'], 'L3_xattn_Wq': _L3_xattn_in['Wq'], 'L3_xattn_Wk': _L3_xattn_in['Wk'], 'L3_xattn_Wv': _L3_xattn_in['Wv'], 'L3_xattn_Wo': _L3_xattn_in['Wo'], 'L3_xattn_bo': _L3_xattn_in['bo'], 'L3_ffn_router_w': _L3_ffn_in['router_w'], 'L3_ffn_router_b': _L3_ffn_in['router_b'], 'L3_ffn_w1': _L3_ffn_in['w1'], 'L3_ffn_b1': _L3_ffn_in['b1'], 'L3_ffn_w2': _L3_ffn_in['w2'], 'L3_ffn_b2': _L3_ffn_in['b2']}

def reference(x, ctx_1024, mask_Bx1xS2_ik0, mask_Bx1xSxS2_ik1, g_xattn, g_ffn, L0_xattn_Wu, L0_xattn_Wv, L0_ffn_gate_w, L0_ffn_wg, L0_ffn_wu, L0_ffn_wd, L0_ffn_swg, L0_ffn_swu, L0_ffn_swd, L1_xattn_Wq, L1_xattn_bq, L1_ffn_ln_g, L1_ffn_ln_b, L1_ffn_router_w, L1_ffn_up_W, L1_ffn_up_b, L1_ffn_down_W, L1_ffn_down_b, L1_ffn_spec0_W, L1_ffn_spec0_b, L1_ffn_ln0_g, L1_ffn_ln0_b, L1_ffn_spec1a_W, L1_ffn_spec1a_b, L1_ffn_spec1b_W, L1_ffn_spec1b_b, L1_ffn_ln1_g, L1_ffn_ln1_b, L1_ffn_spec2_W, L1_ffn_spec2_b, L2_xattn_W, L2_xattn_b, L2_ffn_w_gate, L2_ffn_w_up, L2_ffn_w_down, L3_xattn_Wq, L3_xattn_Wk, L3_xattn_Wv, L3_xattn_Wo, L3_xattn_bo, L3_ffn_router_w, L3_ffn_router_b, L3_ffn_w1, L3_ffn_b1, L3_ffn_w2, L3_ffn_b2):
    import jax
    import jax.numpy as jnp

    def _L0_xattn_ref(q, k, v, Wu, Wv):
        import jax, jax.numpy as jnp
        import numpy as np
        B, N, D, R = (4, 512, 128, 32)
        rank = Wu.shape[-1]
        u = jnp.einsum('bnd,dr->bnr', q, Wu)
        vp = jnp.einsum('bnd,dr->bnr', k, Wv)
        scores = jnp.einsum('bnr,bmr->bnm', u, vp)
        attn = jax.nn.softmax(scores / jnp.sqrt(jnp.float32(rank)), axis=-1)
        out = jnp.einsum('bnm,bmd->bnd', attn, v)
        return out

    def _L0_ffn_ref(x, gate_w, wg, wu, wd, swg, swu, swd):
        import jax, jax.numpy as jnp
        import numpy as np
        HIDDEN = 128
        N_EXPERTS = 8
        TOP_K = 2
        INTER = 176
        N_SHARED = 2
        SCALE = 1.0
        B, S, H = x.shape
        xf = x.reshape(-1, H)
        T = xf.shape[0]
        logits = xf.astype(jnp.float32) @ gate_w.astype(jnp.float32).T
        scores = jax.nn.softmax(logits, axis=-1)
        topw, topi = jax.lax.top_k(scores, TOP_K)
        denom = topw.sum(axis=-1, keepdims=True) + 1e-20
        topw = topw / denom * SCALE
        wdense = jnp.zeros((T, N_EXPERTS), jnp.float32).at[jnp.arange(T)[:, None], topi].set(topw)
        hg = jnp.einsum('th,ehi->eti', xf, wg)
        hu = jnp.einsum('th,ehi->eti', xf, wu)
        eo = jnp.einsum('eti,eih->eth', jax.nn.silu(hg) * hu, wd)
        y = jnp.einsum('te,eth->th', wdense, eo)
        shared = jax.nn.silu(xf @ swg) * (xf @ swu) @ swd
        return (y + shared).reshape(B, S, H)

    def _L1_xattn_ref(query, key, value, mask, Wq, bq):
        import jax, jax.numpy as jnp
        import numpy as np
        import math
        N_HEAD = 16
        N_FEAT = 128
        D_K = N_FEAT // N_HEAD
        B, T1, _ = query.shape
        T2 = key.shape[1]
        q = (jnp.einsum('btf,gf->btg', query, Wq) + bq).reshape(B, T1, N_HEAD, D_K).transpose(0, 2, 1, 3)
        k = key.reshape(B, T2, N_HEAD, D_K).transpose(0, 2, 1, 3)
        v = value.reshape(B, T2, N_HEAD, D_K).transpose(0, 2, 1, 3)
        scores = jnp.einsum('bhqd,bhkd->bhqk', q, k) / math.sqrt(D_K)
        m = mask[:, None, :, :] == 0
        min_value = jnp.finfo(scores.dtype).min
        scores = jnp.where(m, min_value, scores)
        attn = jax.nn.softmax(scores, axis=-1)
        attn = jnp.where(m, 0.0, attn)
        x = jnp.einsum('bhqk,bhkd->bhqd', attn, v)
        return x.transpose(0, 2, 1, 3).reshape(B, T1, N_FEAT)

    def _L1_ffn_ref(hidden_states, ln_g, ln_b, router_w, up_W, up_b, down_W, down_b, spec0_W, spec0_b, ln0_g, ln0_b, spec1a_W, spec1a_b, spec1b_W, spec1b_b, ln1_g, ln1_b, spec2_W, spec2_b):
        import jax, jax.numpy as jnp
        import numpy as np
        B, S, H, F, E, K = (2, 256, 128, 512, 8, 2)

        def _ln(x, g, b, eps=1e-05):
            m = jnp.mean(x, axis=-1, keepdims=True)
            v = jnp.var(x, axis=-1, keepdims=True)
            return (x - m) / jnp.sqrt(v + eps) * g + b

        def _gelu(x):
            return jax.nn.gelu(x, approximate=False)
        b, s, h = hidden_states.shape
        x = hidden_states.reshape(-1, h)
        nx = _ln(x, ln_g, ln_b)
        logits = nx @ router_w
        probs = jax.nn.softmax(logits, axis=-1)
        _, idx = jax.lax.top_k(probs, K)
        mask = jnp.sum(jax.nn.one_hot(idx, probs.shape[-1], dtype=probs.dtype), axis=1)
        w = probs * mask
        w = w / jnp.sum(w, axis=-1, keepdims=True)
        h1 = _gelu(jnp.einsum('th,ehf->etf', nx, up_W) + up_b[:, None, :])
        i0 = jnp.array([0, 4])
        i1 = jnp.array([1, 5])
        i2 = jnp.array([2, 6])
        s0 = _gelu(_ln(jnp.einsum('etf,efg->etg', h1[i0], spec0_W) + spec0_b[:, None, :], ln0_g[:, None, :], ln0_b[:, None, :]))
        t1 = _gelu(jnp.einsum('etf,efg->etg', h1[i1], spec1a_W) + spec1a_b[:, None, :])
        s1 = _ln(jnp.einsum('etg,egf->etf', t1, spec1b_W) + spec1b_b[:, None, :], ln1_g[:, None, :], ln1_b[:, None, :])
        s2 = _gelu(jnp.einsum('etf,efg->etg', h1[i2], spec2_W) + spec2_b[:, None, :])
        h2 = h1.at[i0].set(s0).at[i1].set(s1).at[i2].set(s2)
        out_e = jnp.einsum('etf,efh->eth', h2, down_W) + down_b[:, None, :]
        y = jnp.einsum('eth,te->th', out_e, w) + x
        return y.reshape(hidden_states.shape)

    def _L2_xattn_ref(x1, x2, W, b):
        import jax, jax.numpy as jnp
        import numpy as np
        D1, D2, D3 = (128, 128, 128)
        d1 = x1.shape[-1]
        W1 = W[:, :d1]
        W2 = W[:, d1:]
        part1 = jnp.einsum('bld,ed->ble', x1, W1)
        part2 = jnp.einsum('bld,ed->be', x2, W2) / x2.shape[1]
        return part1 + part2[:, None, :] + b

    def _L2_ffn_ref(x, w_gate, w_up, w_down):
        import jax, jax.numpy as jnp
        import numpy as np
        BLOCK = 16
        _GRID = jnp.array([0.0, 0.5, 1.0, 1.5, 2.0, 3.0, 4.0, 6.0], dtype=jnp.float32)
        _MID = jnp.array([0.25, 0.75, 1.25, 1.75, 2.5, 3.5, 5.0], dtype=jnp.float32)

        def fp4_quant_dequant(x):
            shape = x.shape
            xb = x.reshape(shape[:-1] + (shape[-1] // BLOCK, BLOCK))
            scale = jnp.max(jnp.abs(xb), axis=-1, keepdims=True) / 6.0
            scale = jnp.maximum(scale, jnp.float32(1e-12))
            xn = xb / scale
            idx = jnp.searchsorted(_MID, jnp.abs(xn))
            q = _GRID[idx] * jnp.sign(xn) * scale
            return q.reshape(shape)

        def fp4_linear(x, w):
            xq = fp4_quant_dequant(x)
            wq = fp4_quant_dequant(w)
            return jnp.einsum('bsk,nk->bsn', xq, wq)
        gate = fp4_linear(x, w_gate)
        y = fp4_linear(x, w_up)
        h = jax.nn.silu(gate) * y
        return fp4_linear(h, w_down)

    def _L3_xattn_ref(query, keys, values, mask, Wq, Wk, Wv, Wo, bo):
        import jax, jax.numpy as jnp
        import numpy as np
        EMBED_SIZE = 128
        HEADS = 16
        HEAD_DIM = EMBED_SIZE // HEADS
        N, Q = (query.shape[0], query.shape[1])
        K = keys.shape[1]
        q = query.reshape(N, Q, HEADS, HEAD_DIM)
        k = keys.reshape(N, K, HEADS, HEAD_DIM)
        v = values.reshape(N, K, HEADS, HEAD_DIM)
        q = jnp.einsum('nqhd,ed->nqhe', q, Wq)
        k = jnp.einsum('nkhd,ed->nkhe', k, Wk)
        v = jnp.einsum('nkhd,ed->nkhe', v, Wv)
        energy = jnp.einsum('nqhd,nkhd->nhqk', q, k)
        energy = jnp.where(mask == 0, jnp.float32(-10000000000.0), energy)
        attn = jax.nn.softmax(energy / jnp.sqrt(jnp.float32(EMBED_SIZE)), axis=3)
        out = jnp.einsum('nhqk,nkhd->nqhd', attn, v).reshape(N, Q, EMBED_SIZE)
        return out @ Wo.T + bo

    def _L3_ffn_ref(x, router_w, router_b, w1, b1, w2, b2):
        import jax, jax.numpy as jnp
        import numpy as np
        NEG_INF = -1e+30

        def _moe_forward(x, router_w, router_b, w1, b1, w2, b2, top_k=2):
            B, S, D = x.shape
            E = router_w.shape[1]
            logits = jnp.einsum('bsd,de->bse', x, router_w) + router_b
            top_vals, top_idx = jax.lax.top_k(logits, top_k)
            keep = jax.nn.one_hot(top_idx, E, dtype=logits.dtype).sum(-2) > 0
            sparse_logits = jnp.where(keep, logits, NEG_INF)
            gating = jax.nn.softmax(sparse_logits, axis=-1)
            xf = x.reshape(-1, D)
            gf = gating.reshape(-1, E)
            h = jax.nn.relu(jnp.einsum('td,edh->eth', xf, w1) + b1[:, None, :])
            y = jnp.einsum('eth,ehd->etd', h, w2) + b2[:, None, :]
            out = jnp.einsum('etd,te->td', y, gf)
            return out.reshape(B, S, D)
        return _moe_forward(x, router_w, router_b, w1, b1, w2, b2, top_k=2)
    x = x + jnp.tanh(g_xattn[0]) * _L0_xattn_ref(_layernorm(x, axis=-1), ctx_1024, ctx_1024, L0_xattn_Wu, L0_xattn_Wv)
    x = x + jnp.tanh(g_ffn[0]) * _L0_ffn_ref(_layernorm(x, axis=-1), L0_ffn_gate_w, L0_ffn_wg, L0_ffn_wu, L0_ffn_wd, L0_ffn_swg, L0_ffn_swu, L0_ffn_swd)
    x = x + jnp.tanh(g_xattn[1]) * _L1_xattn_ref(_layernorm(x, axis=-1), ctx_1024, ctx_1024, mask_Bx1xS2_ik0, L1_xattn_Wq, L1_xattn_bq)
    x = x + jnp.tanh(g_ffn[1]) * _L1_ffn_ref(_layernorm(x, axis=-1), L1_ffn_ln_g, L1_ffn_ln_b, L1_ffn_router_w, L1_ffn_up_W, L1_ffn_up_b, L1_ffn_down_W, L1_ffn_down_b, L1_ffn_spec0_W, L1_ffn_spec0_b, L1_ffn_ln0_g, L1_ffn_ln0_b, L1_ffn_spec1a_W, L1_ffn_spec1a_b, L1_ffn_spec1b_W, L1_ffn_spec1b_b, L1_ffn_ln1_g, L1_ffn_ln1_b, L1_ffn_spec2_W, L1_ffn_spec2_b)
    x = x + jnp.tanh(g_xattn[2]) * _L2_xattn_ref(_layernorm(x, axis=-1), ctx_1024, L2_xattn_W, L2_xattn_b)
    x = x + jnp.tanh(g_ffn[2]) * _L2_ffn_ref(_layernorm(x, axis=-1), L2_ffn_w_gate, L2_ffn_w_up, L2_ffn_w_down)
    x = x + jnp.tanh(g_xattn[3]) * _L3_xattn_ref(_layernorm(x, axis=-1), ctx_1024, ctx_1024, mask_Bx1xSxS2_ik1, L3_xattn_Wq, L3_xattn_Wk, L3_xattn_Wv, L3_xattn_Wo, L3_xattn_bo)
    x = x + jnp.tanh(g_ffn[3]) * _L3_ffn_ref(_layernorm(x, axis=-1), L3_ffn_router_w, L3_ffn_router_b, L3_ffn_w1, L3_ffn_b1, L3_ffn_w2, L3_ffn_b2)
    return x

_drawn_inputs = setup_inputs


def setup_inputs(seed=0):
    import zlib

    import numpy as np

    out = dict(_drawn_inputs(seed))
    spreads = {'L1_ffn_ln_g': (1.0, 0.2),
     'L1_ffn_ln_b': (0.0, 0.1),
     'L1_ffn_up_b': (0.0, 0.651),
     'L1_ffn_down_b': (0.0, 0.1),
     'L1_ffn_spec0_b': (0.0, 0.1),
     'L1_ffn_ln0_g': (1.0, 0.6),
     'L1_ffn_ln0_b': (0.0, 0.8),
     'L1_ffn_spec1a_b': (0.0, 0.629),
     'L1_ffn_spec1b_b': (0.0, 0.1),
     'L1_ffn_ln1_g': (1.0, 0.6),
     'L1_ffn_ln1_b': (0.0, 0.8),
     'L1_ffn_spec2_b': (0.0, 0.8),
     'L3_ffn_router_b': (0.0, 0.347),
     'L3_ffn_b1': (0.0, 2.0),
     'L3_ffn_b2': (0.0, 0.87)}
    factors = {'g_ffn': 18.51,
     'L1_ffn_spec1a_W': 7.346,
     'L1_ffn_spec1b_W': 4.009,
     'L1_ffn_spec2_W': 8.0,
     'L2_xattn_b': 4.234,
     'L2_ffn_w_gate': 8.0,
     'L2_ffn_w_up': 8.0,
     'L2_ffn_w_down': 8.0,
     'L3_xattn_bo': 50.754,
     'L3_ffn_w1': 9.165,
     'L3_xattn_Wq': 6.204,
     'L3_xattn_Wk': 6.349}
    for name, (base, spread) in spreads.items():
        noise = np.random.default_rng([zlib.crc32(name.encode()), seed]).standard_normal(out[name].shape)
        drawn = base * np.exp(spread * noise) if base else spread * noise
        out[name] = jnp.asarray(drawn.astype(out[name].dtype))
    for name, factor in factors.items():
        out[name] = (out[name] * factor).astype(out[name].dtype)
    return out
```

```python
import numpy as np
import concourse.bass as bass
from concourse import mybir
from contextlib import ExitStack

B, S, D = 8, 128, 128
T = B * S
KC = 77
NH, DK = 16, 8
R0 = 32
E = 8
HALF = 512
TH = HALF // S
I0, C0 = 176, 88
F1, F2 = 512, 256
F3 = 512
I2 = 352
QB = 16
EPS = 1e-5
MASKED = -1.0e30
UNIT = 3072
NRING = 4


def plan():
    stages, n = [], dict(job=0, act=0, dve=0, hid=0, down=0, norm=0)
    consumers = []

    def add(layer, kind, e, h, unit, jobs="", hid=0, down=0, norm=0):
        stages.append(dict(layer=layer, kind=kind, e=e, h=h, unit=unit, job=n["job"], hid=n["hid"],
                           down=n["down"], norm=n["norm"], act=n["act"], dve=n["dve"]))
        for c in jobs:
            eng = "act" if c == "A" else "dve"
            n[eng] += 1
            consumers.append((eng, n[eng]))
            n["job"] += 1
        n["hid"] += hid
        n["down"] += down
        n["norm"] += norm

    unit = 0
    for layer in (0, 1, 3):
        count = 10 if layer == 0 else 8
        up = ("up", dict(jobs="AD" * 2, hid=2)) if layer == 0 else ("up", dict(jobs="AAAA", hid=4))
        for h in range(2):
            add(layer, up[0], 0, h, unit, **up[1])
        for e in range(count):
            kind = e % 4 if layer == 1 else 3
            if kind == 0:
                for h in range(2):
                    add(layer, "spec0", e, h, unit, jobs="DDDD", norm=4)
            elif kind == 1:
                for h in range(2):
                    add(layer, "spec1a", e, h, unit, jobs="AA", hid=2)
                for h in range(2):
                    add(layer, "spec1b", e, h, unit, jobs="DDDD", norm=4)
            elif kind == 2:
                for h in range(2):
                    add(layer, "spec2", e, h, unit, jobs="AAAA", hid=4)
            if kind < 2:
                for h in range(2):
                    add(layer, "turn", e, h, unit, jobs="AAAA", hid=4)
            for h in range(2):
                add(layer, "down", e, h, unit, down=1)
                if e + 1 < count:
                    add(layer, up[0], e + 1, h, unit + 1, **up[1])
            unit += 1
        if layer != 0:
            for h in range(2):
                add(layer, "bias", count, h, unit - 1, down=1)
    return stages, consumers, unit


def program(nc, a, out):
    fp32, fp32r = mybir.dt.float32, mybir.dt.float32r
    bf16, i32, u32 = mybir.dt.bfloat16, mybir.dt.int32, mybir.dt.uint32
    ALU, ACT, AX = mybir.AluOpType, mybir.ActivationFunctionType, mybir.AxisListType
    STAGES, CONSUMERS, NUNITS = plan()

    def stages_of(layer):
        return [s for s in STAGES if s["layer"] == layer]

    def unit_parts(u):
        if u < 10:
            if u < E:
                g, w, d = a["L0_ffn_wg"][u], a["L0_ffn_wu"][u], a["L0_ffn_wd"][u]
            else:
                c = slice((u - E) * I0, (u - E + 1) * I0)
                g, w, d = a["L0_ffn_swg"][:, c], a["L0_ffn_swu"][:, c], a["L0_ffn_swd"][c, :]
            return [(128, 0, I0, g), (128, I0, I0, w),
                    (C0, 2 * I0, 2 * D, d.rearrange("(c p) h -> p c h", p=C0))]
        if u < 10 + E:
            e = u - 10
            parts = [(128, 0, F1, a["L1_ffn_up_W"][e])]
            g = e // 4
            if e % 4 == 0:
                parts.append((128, F1, 4 * F1, a["L1_ffn_spec0_W"][g].rearrange("(c p) f -> p c f", p=128)))
            elif e % 4 == 1:
                parts.append((128, F1, 4 * F2, a["L1_ffn_spec1a_W"][g].rearrange("(c p) f -> p c f", p=128)))
                parts.append((128, F1 + 4 * F2, 2 * F1,
                              a["L1_ffn_spec1b_W"][g].rearrange("(c p) f -> p c f", p=128)))
            elif e % 4 == 2:
                parts.append((128, F1, 4 * F1, a["L1_ffn_spec2_W"][g].rearrange("(c p) f -> p c f", p=128)))
            at = parts[-1][1] + parts[-1][2]
            parts.append((128, at, 4 * D, a["L1_ffn_down_W"][e].rearrange("(c p) h -> p c h", p=128)))
            return parts
        e = u - 10 - E
        return [(128, 0, F3, a["L3_ffn_w1"][e]),
                (128, F3, 4 * D, a["L3_ffn_w2"][e].rearrange("(c p) h -> p c h", p=128))]

    PARTS = [unit_parts(u) for u in range(NUNITS)]
    LOADED = []
    for u in range(NUNITS):
        LOADED.append((LOADED[u - 2] if u >= 2 else 0) + 16 * len(PARTS[u]))

    def down_at(u):
        return PARTS[u][-1][1]

    ctx = ExitStack()
    with ctx:
        def sb(name, shape, dt=fp32):
            return ctx.enter_context(nc.sbuf_tensor(name, shape, dt))

        def sem(name):
            return ctx.enter_context(nc.semaphore(name))

        X = sb("X", [128, B, D])
        XN = sb("XN", [128, B, D])
        XT = sb("XT", [128, T])
        XTh = sb("XTh", [128, T], fp32r)
        XTl = sb("XTl", [128, T], fp32r)
        ctx_at = nc.sbuf_base
        CTX = sb("CTX", [KC, B, D])
        CT = sb("CT", [128, B * KC])
        V1 = sb("V1", [KC, B, NH * (DK + 1)])
        RAW = sb("RAW", [128, 2, UNIT])
        WH = sb("WH", [128, 2, UNIT], fp32r)
        WL = sb("WL", [128, 2, UNIT], fp32r)
        hidden_at = nc.sbuf_base
        hidden_bytes = 2 * 4 * HALF * 4
        H1h = sb("H1h", [128, 2, 4 * HALF], fp32r)
        H1l = sb("H1l", [128, 2, 4 * HALF], fp32r)
        H2h = sb("H2h", [128, 2, 4 * HALF], fp32r)
        H2l = sb("H2l", [128, 2, 4 * HALF], fp32r)

        def over(name, i, shape):
            return nc.alloc_sbuf_tensor_at(name, shape, fp32, offset=hidden_at + i * hidden_bytes)

        G = sb("G", [128, 4, HALF])
        turned_at = nc.sbuf_base
        SN = sb("SN", [128, 2, 4 * HALF])
        XM = nc.alloc_sbuf_tensor_at("XM", [128, B, D], fp32, offset=turned_at)
        WGT = nc.alloc_sbuf_tensor_at("WGT", [E, T], fp32, offset=turned_at + 4 * T)
        BDK = nc.alloc_sbuf_tensor_at("BDK", [128, 2, NH * KC], fp32, offset=turned_at)
        SG = SN[:, 0, :].rearrange("p (s n) -> p s n", s=4)
        ATT = over("ATT", 0, [128, 8 * HALF])
        ATT3 = over("ATT3", 1, [128, 8 * HALF])
        ATT2 = over("ATT2", 2, [128, 8 * HALF])
        QT = ATT[:, 0:T]
        SUB = ATT[:, 1024:1024 + NH * KC]
        PB = ATT[:, 2304:2304 + NH * KC]
        PT = ATT2[0:KC, 0:NH * S]
        ON = ATT2[:, 2048:3072]
        TMP = ATT3[:, 0:D]
        ONT = ATT3[:, 1024:2048]
        K3T = ATT3[:, 2048:2048 + B * KC]
        U0T = ATT[0:R0, 0:T]
        VP0 = ATT3[0:R0, 0:B * KC]
        CSB = ATT2[:, 0:T]
        QA = ATT[:, 0:T]
        QC = ATT[:, 1024:2048]
        QD = ATT[:, 2048:3072]
        XQ = ATT2[:, 0:T]
        HG = ATT2[:, 1024:1024 + 2 * I2]
        HQ = ATT2[:, 2048:2048 + 2 * I2]
        HQT = ATT3[:, 0:2 * 3 * S]
        ident = sb("ident", [128, 128])
        identb = sb("identb", [128, 128], bf16)
        ones = sb("ones", [1, 128])
        onesr = sb("onesr", [33, 128], fp32r)
        HM = sb("HM", [128, NH])
        REV = sb("REV", [128, B, E])
        TG = sb("TG", [128, 8])
        GB = sb("GB", [128, 8])
        Wu = sb("Wu", [128, R0])
        Wv = sb("Wv", [128, R0])
        GW0 = sb("GW0", [128, E])
        WQ1 = sb("WQ1", [128, D])
        BQ1 = sb("BQ1", [128, 1])
        LNG = sb("LNG", [128, 2])
        RW1 = sb("RW1", [128, E])
        UB1 = sb("UB1", [128, 4 * E])
        SB1 = sb("SB1", [128, 2 * (2 + 4)])
        LG1 = sb("LG1", [128, 4 * 4])
        LB1 = sb("LB1", [128, 4 * 4])
        ROW = over("ROW", 3, [33, 4 * F1])
        ROWr = sb("ROWr", [33, 4 * F1], fp32r)
        DB1 = sb("DB1", [E, D])
        W2A = nc.alloc_sbuf_tensor_at("W2A", [128, 2 * D], fp32, offset=hidden_at + 2 * hidden_bytes + 4 * 3712)
        B2A = sb("B2A", [1, D])
        W2R = nc.alloc_sbuf_tensor_at("W2R", [128, 3, 3, D], fp32, offset=turned_at + 10240)
        W2Q = over("W2Q", 3, [128, 2 * I2 + 3 * D])
        WQK = sb("WQK", [128, 3 * DK])
        BD3 = nc.alloc_sbuf_tensor_at("BD3", [128, 3, D], fp32, offset=hidden_at + 2 * hidden_bytes + 4 * 3072)
        WO3 = sb("WO3", [128, D])
        BO3 = sb("BO3", [1, D])
        RW3 = sb("RW3", [128, E])
        RB3 = sb("RB3", [128, E])
        FB3 = sb("FB3", [128, 4 * E])
        DB3 = sb("DB3", [E, D])
        MI = nc.alloc_sbuf_tensor_at("MI", [128, B * KC], i32, offset=hidden_at + hidden_bytes + 4 * 2752)
        MB1 = sb("MB1", [128, B * KC], bf16)
        MB3 = nc.alloc_sbuf_tensor_at("MB3", [128, B * KC], bf16, offset=ctx_at + 4 * 10 * B * E)
        ANY = sb("ANY", [128, B])
        CS = sb("CS", [128, B])
        ST = sb("ST", [128, B, 6])
        MV = sb("MV", [128, B, 2])
        VE = sb("VE", [128, B])
        RSTD = sb("RSTD", [128, B])
        MHALF = sb("MHALF", [128, B])
        MX = sb("MX", [128, NH])
        RC = sb("RC", [128, NH])
        RC2 = sb("RC2", [128, NH])
        RT = nc.alloc_sbuf_tensor_at("RT", [128, 10, B * E], fp32, offset=ctx_at)
        RM = sb("RM", [128, 4, B])
        WG = sb("WG", [128, 3, B * E])
        QS = nc.alloc_sbuf_tensor_at("QS", [128, 3, 64], fp32, offset=hidden_at + 2 * hidden_bytes + 4 * 3520)

        PS = [ctx.enter_context(nc.psum_tensor(f"PS{i}", [128, HALF], fp32)) for i in range(8)]

        in_x, in_ctx, in_small = sem("in_x"), sem("in_ctx"), sem("in_small")
        in_w2 = sem("in_w2")
        mask1_in, mask3_in = sem("mask1_in"), sem("mask3_in")
        raw_loaded = [sem("raw_loaded0"), sem("raw_loaded1")]
        pool_const, pool_step = sem("pool_const"), sem("pool_step")
        dve_step, act_step = sem("dve_step"), sem("act_step")
        const_copied = sem("const_copied")
        var_ready, rstd_ready, xn_ready = sem("var_ready"), sem("rstd_ready"), sem("xn_ready")
        xnt_full, xt_ready, xtl_ready = sem("xnt_full"), sem("xt_ready"), sem("xtl_ready")
        ctxt_full, ct_ready = sem("ctxt_full"), sem("ct_ready")
        tg_ready = sem("tg_ready")
        a0_up, a0_upc, a0_s, a0_sub, a0_exp = sem("a0_up"), sem("a0_upc"), sem("a0_s"), sem("a0_sub"), sem("a0_exp")
        a0_pt, a0_ptc, a0_o = sem("a0_pt"), sem("a0_ptc"), sem("a0_o")
        q_full, q_ready = sem("q_full"), sem("q_ready")
        v1_ready, k3_full, k3_ready, v3_full, v3_ready = (sem("v1_ready"), sem("k3_full"), sem("k3_ready"),
                                                          sem("v3_full"), sem("v3_ready"))
        bd3_ready = sem("bd3_ready")
        bdk_ready, s_full, sub_done, exp_done = sem("bdk_ready"), sem("s_full"), sem("sub_done"), sem("exp_done")
        pt_full, pt_act, pt_dve, o_full, o_done = sem("pt_full"), sem("pt_act"), sem("pt_dve"), sem("o_full"), sem("o_done")
        ont_full, ont_ready, wo_full = sem("ont_full"), sem("ont_ready"), sem("wo_full")
        csb_ready, a2_full = sem("csb_ready"), sem("a2_full")
        logit_full, dif_ready, gate_exp = sem("logit_full"), sem("dif_ready"), sem("gate_exp")
        wg_ready, wgt_full, wgt_ready = sem("wg_ready"), sem("wgt_full"), sem("wgt_ready")
        hi_done, lo_done, unit_used = sem("hi_done"), sem("lo_done"), sem("unit_used")
        ring_full, act_freed, dve_freed = sem("ring_full"), sem("act_freed"), sem("dve_freed")
        split_done, down_full, down_free = sem("split_done"), sem("down_full"), sem("down_free")
        tvar_ready, trstd_ready, norm_done = sem("tvar_ready"), sem("trstd_ready"), sem("norm_done")
        wq_ready, wq_full, wq_copied, xq_ready = sem("wq_ready"), sem("wq_full"), sem("wq_copied"), sem("xq_ready")
        f2_up, f2_silu, f2_q, f2_t, f2_tc, f2_down = (sem("f2_up"), sem("f2_silu"), sem("f2_q"), sem("f2_t"),
                                                      sem("f2_tc"), sem("f2_down"))
        f2_used = sem("f2_used")
        row_ready = sem("row_ready")
        stored = sem("stored")

        SMALL = [
            (Wu[:, :], a["L0_xattn_Wu"]), (Wv[:, :], a["L0_xattn_Wv"]),
            (GB[:, 0:4], a["g_xattn"].partition_broadcast(128)),
            (GB[:, 4:8], a["g_ffn"].partition_broadcast(128)),
            (GW0[:, :], a["L0_gate_T"]), (WQ1[:, :], a["L1_Wq_T"]), (BQ1[:, :], a["L1_bq_col"]),
            (LNG[:, 0:1], a["L1_ln_g_col"]), (LNG[:, 1:2], a["L1_ln_b_col"]),
            (RW1[:, :], a["L1_ffn_router_w"]), (UB1[:, :], a["L1_up_b_cols"]),
            (SB1[:, 0:4], a["L1_spec1a_b_cols"]), (SB1[:, 4:12], a["L1_spec2_b_cols"]),
            (LG1[:, 0:8], a["L1_ln0_g_cols"]), (LG1[:, 8:16], a["L1_ln1_g_cols"]),
            (LB1[:, 0:8], a["L1_ln0_b_cols"]), (LB1[:, 8:16], a["L1_ln1_b_cols"]),
            (DB1[:, :], a["L1_ffn_down_b"]), (B2A[:, :], a["L2_b_row"]),
            (WQK[:, :], a["L3_WqkvT_heads"]), (WO3[:, :], a["L3_Wo_T"]), (BO3[:, :], a["L3_bo_row"]),
            (RW3[:, :], a["L3_ffn_router_w"]), (RB3[:, :], a["L3_ffn_router_b"].partition_broadcast(128)),
            (FB3[:, :], a["L3_b1_cols"]), (DB3[:, :], a["L3_ffn_b2"]),
        ]
        for p in (0, 32):
            SMALL.append((ROW[p:p + 1, 0:2 * F1], a["L1_spec0_b_row"]))
            SMALL.append((ROW[p:p + 1, 2 * F1:4 * F1], a["L1_spec1b_b_row"]))
        LAYER2 = [(W2A[:, :], a["L2_W_T"])]
        for m, name in enumerate(("L2_ffn_w_gate", "L2_ffn_w_up")):
            for c in range(3):
                k = min(128, I2 - 128 * c)
                LAYER2.append((W2R[0:k, m, c, :], a[name][128 * c:128 * c + k, :]))
        LAYER2.append((W2R[:, 2, :, :].rearrange("p c k -> p (c k)")[:, 0:I2], a["L2_ffn_w_down"]))
        SMALL_IN = 16 * len(SMALL)

        block = ctx.enter_context(nc.Block())

        @block.sync
        def _(sp):
            sp.dma_start(X[:, :, :], a["x"].rearrange("b p d -> p b d")).then_inc(in_x, 16)
            sp.dma_start(CTX[:, :, :], a["ctx_1024"].rearrange("b k d -> k b d")).then_inc(in_ctx, 16)
            sp.dma_start(MI[:, :], a["mask_Bx1xS2_ik0"].rearrange("b o k -> (b o k)")
                         .partition_broadcast(128)).then_inc(mask1_in, 16)
            for u in range(NUNITS):
                if u >= 2:
                    sp.wait_ge(lo_done, u - 1)
                for p, c, n, src in PARTS[u]:
                    dst = RAW[0:p, u % 2, c:c + n]
                    if len(src.shape) == 3:
                        dst = dst.rearrange("p (c n) -> p c n", c=src.shape[1])
                    sp.dma_start(dst, src).then_inc(raw_loaded[u % 2], 16)
                if u == 19:
                    sp.wait_ge(unit_used, 18)
                    for dst, src in LAYER2:
                        sp.dma_start(dst, src).then_inc(in_w2, 16)
                    sp.dma_start(MI[:, :].rearrange("q (b k) -> q b k", b=B),
                                 a["mask_Bx1xSxS2_ik1"].rearrange("b o q k -> q (b o) k")).then_inc(mask3_in, 16)
            sp.wait_ge(down_free, STAGES[-1]["down"] + 1)
            sp.dma_start(out.rearrange("b p d -> p b d"), X[:, :, :]).then_inc(stored, 16)
            sp.wait_ge(stored, 16)

        @block.gpsimd
        def _(pool):
            steps = [0]

            def step(ins):
                steps[0] += 1
                ins.then_inc(pool_step, 1)
                pool.wait_ge(pool_step, steps[0])

            g = nc.gpsimd
            step(g.memset(ident[:, :], 0.0))
            g.affine_select(out=ident[:, :], in_=ident[:, :], compare_op=ALU.not_equal, fill=1.0, base=0,
                            pattern=[[-1, 128]], channel_multiplier=1).then_inc(pool_const, 1)
            g.memset(ones[:, :], 1.0).then_inc(pool_const, 1)
            g.memset(onesr[:, :].bitcast(fp32), 1.0).then_inc(pool_const, 1)
            step(g.memset(HM[:, :], 1.0))
            step(g.affine_select(out=HM[:, :], in_=HM[:, :], compare_op=ALU.is_ge, fill=0.0, base=0,
                                 pattern=[[-DK, NH]], channel_multiplier=1))
            g.affine_select(out=HM[:, :], in_=HM[:, :], compare_op=ALU.is_ge, fill=0.0, base=DK - 1,
                            pattern=[[DK, NH]], channel_multiplier=-1).then_inc(pool_const, 1)
            g.memset(MHALF[:, :], -0.5).then_inc(pool_const, 1)
            for e in range(E):
                last = g.memset(REV[:, :, e:e + 1], float(E - e))
            last.then_inc(pool_const, 1)
            pool.wait_ge(pool_const, 6)

            def rstd(n):
                pool.wait_ge(var_ready, n + 1)
                g.tensor_tensor(RSTD[:, :], VE[:, :], MHALF[:, :], ALU.pow).then_inc(rstd_ready, 1)

            def low_parts(u, part=None, pieces=1):
                pool.wait_ge(hi_done, u + 1)
                if part is None:
                    for k, c, n, _ in PARTS[u]:
                        last = g.tensor_tensor(WL[0:k, u % 2, c:c + n], RAW[0:k, u % 2, c:c + n],
                                               WH[0:k, u % 2, c:c + n].bitcast(fp32), ALU.subtract)
                    last.then_inc(lo_done, 1)
                    return
                total = PARTS[u][-1][1] + PARTS[u][-1][2]
                c, e = total * part // pieces, total * (part + 1) // pieces
                last = g.tensor_tensor(WL[:, u % 2, c:e], RAW[:, u % 2, c:e],
                                       WH[:, u % 2, c:e].bitcast(fp32), ALU.subtract)
                if part == pieces - 1:
                    last.then_inc(lo_done, 1)

            def head_keys(layer, kt):
                first = 0 if layer == 1 else B
                for b in range(first, first + B):
                    if b >= 2:
                        pool.wait_ge(s_full, 3 * (b - 1))
                    keys = kt[:, (b - first) * KC:(b - first + 1) * KC].rearrange("p (o k) -> p o k", o=1)
                    heads = HM[:, :].rearrange("p (h o) -> p h o", o=1)
                    g.tensor_tensor(BDK[:, b % 2, :].rearrange("p (h k) -> p h k", h=NH),
                                    keys.to_broadcast([128, NH, KC]), heads.to_broadcast([128, NH, KC]),
                                    ALU.mult).then_inc(bdk_ready, 1)

            rstd(0)
            low_parts(0)
            pool.wait_ge(in_ctx, 16)
            step(g.memset(V1[:, :, :], 1.0))
            g.tensor_copy(V1[:, :, :].rearrange("k b (h d) -> k b h d", h=NH)[:, :, :, 0:DK],
                          CTX[:, :, :].rearrange("k b (h d) -> k b h d", h=NH)).then_inc(v1_ready, 1)
            rstd(1)
            for u in range(1, 11):
                low_parts(u)
            rstd(2)
            pool.wait_ge(ct_ready, 2)
            head_keys(1, CT)
            rstd(3)
            rstd(4)
            for e in range(E):
                u = 10 + e
                if e % 4 < 2:
                    norm = next(s["norm"] for s in STAGES if s["unit"] == u and s["norm"] is not None
                                and s["kind"] in ("spec0", "spec1b"))
                    for t in range(2 * TH):
                        pool.wait_ge(tvar_ready, norm + t + 1)
                        g.tensor_tensor(RSTD[:, t:t + 1], VE[:, t:t + 1], MHALF[:, 0:1], ALU.pow).then_inc(trstd_ready, 1)
                        if t < 6:
                            low_parts(u + 1, t, 6)
                else:
                    low_parts(u + 1)
            rstd(5)
            rstd(6)
            rstd(7)
            pool.wait_ge(k3_ready, 2)
            head_keys(3, K3T)
            rstd(8)
            for u in range(19, NUNITS):
                low_parts(u)

        @block.scalar
        def _(act):
            s = nc.scalar
            for dst, src in SMALL:
                act.dma_start(dst, src).then_inc(in_small, 16)

            def copy(o, i):
                return s.activation(o, i, ACT.Copy)

            def turned(k, split=False, affine=False):
                for h in range(2):
                    act.wait_ge(xnt_full, 2 * k + h + 1)
                    c = slice(h * HALF, (h + 1) * HALF)
                    dsts = [XT[:, c]] + ([XTh[:, c]] if split else [])
                    for d in dsts:
                        if affine:
                            last = s.activation(d, PS[6 + h][:, :], ACT.Identity, scale=LNG[:, 0:1], bias=LNG[:, 1:2])
                        else:
                            last = copy(d, PS[6 + h][:, :])
                    last.then_inc(xt_ready, 1)

            def mixture(layer):
                for st in stages_of(layer):
                    kind, e, h = st["kind"], st["e"], st["h"]
                    if kind == "bias":
                        if h == 0:
                            for i in range(2):
                                n = (0 if layer == 1 else 2) + i
                                act.wait_ge(wgt_full, n + 1)
                                copy(WGT[:, i * HALF:(i + 1) * HALF], PS[6 + i][0:E, :]).then_inc(wgt_ready, 1)
                        continue
                    if kind in ("down", "spec0", "spec1b"):
                        continue
                    if layer == 0:
                        for c in range(2):
                            j = st["job"] + 2 * c
                            act.wait_ge(ring_full, j + 1)
                            k = st["hid"] + c
                            if k >= 4:
                                act.wait_ge(split_done, k - 3)
                            s.activation(SG[0:C0, k % 4, :], PS[j % NRING][0:C0, :], ACT.Silu).then_inc(act_freed, 1)
                        continue
                    for c in range(2 if kind == "spec1a" else 4):
                        j, k = st["job"] + c, st["hid"] + c
                        act.wait_ge(ring_full, j + 1)
                        act.wait_ge(split_done, k - 3)
                        hid = H2h if kind in ("spec1a", "spec2", "turn") else H1h
                        scale = 1.0
                        if layer == 3:
                            func, bias = ACT.Relu, FB3[:, 4 * e + c:4 * e + c + 1]
                        elif kind == "up":
                            func, bias = ACT.Gelu, UB1[:, 4 * e + c:4 * e + c + 1]
                        elif kind == "spec1a":
                            func, bias = ACT.Gelu, SB1[:, 2 * (e // 4) + c:2 * (e // 4) + c + 1]
                        elif kind == "spec2":
                            func, bias = ACT.Gelu, SB1[:, 4 + 4 * (e // 4) + c:5 + 4 * (e // 4) + c]
                        else:
                            at = 8 * (e % 4) + 4 * (e // 4) + c
                            func = ACT.Gelu if e % 4 == 0 else ACT.Identity
                            scale, bias = LG1[:, at:at + 1], LB1[:, at:at + 1]
                        src = PS[j % NRING][:, :]
                        s.activation(G[:, k % 4, :], src, func, bias=bias, scale=scale)
                        s.activation(hid[:, h, c * HALF:(c + 1) * HALF], src, func, bias=bias,
                                     scale=scale).then_inc(act_freed, 1)

            def attention(first, scale):
                for b in range(first, first + B):
                    act.wait_ge(sub_done, b + 1)
                    if b > first:
                        act.wait_ge(pt_full, 4 * b)
                    s.activation(PB, SUB, ACT.Exp, scale=scale).then_inc(exp_done, 1)
                    for i in range(2):
                        act.wait_ge(pt_full, 4 * b + i + 1)
                        copy(PT[:, i * HALF:(i + 1) * HALF], PS[3 + i][0:KC, :]).then_inc(pt_act, 1)

            act.wait_ge(in_small, SMALL_IN)
            s.activation(TG[:, :], GB[:, :], ACT.Tanh).then_inc(tg_ready, 1)
            for i in range(2):
                act.wait_ge(ctxt_full, i + 1)
                copy(CT[:, i * 4 * KC:(i + 1) * 4 * KC], PS[4 + i][:, 0:4 * KC]).then_inc(ct_ready, 1)
            turned(0)
            for i in range(2):
                act.wait_ge(a0_up, i + 1)
                copy(U0T[:, i * HALF:(i + 1) * HALF], PS[i][0:R0, :]).then_inc(a0_upc, 1)
            for i in range(2):
                act.wait_ge(a0_up, i + 3)
                copy(VP0[:, i * 4 * KC:(i + 1) * 4 * KC], PS[2 + i][0:R0, 0:4 * KC]).then_inc(a0_upc, 1)
            for i in range(2):
                act.wait_ge(a0_sub, i + 1)
                c = slice(i * 4 * KC, (i + 1) * 4 * KC)
                s.activation(PB[:, c], SUB[:, c], ACT.Exp, scale=float(R0) ** -0.5).then_inc(a0_exp, 1)
            for i in range(2):
                act.wait_ge(a0_pt, i + 1)
                copy(PT[:, i * HALF:(i + 1) * HALF], PS[6 + i][0:KC, :]).then_inc(a0_ptc, 1)

            def gate(n, d):
                act.wait_ge(dif_ready, n + 1)
                s.activation(RT[:, 1, :], d, ACT.Exp).then_inc(gate_exp, 1)

            turned(1, split=True)
            gate(0, RT[:, 0, :])
            mixture(0)
            turned(2)
            for i in range(2):
                act.wait_ge(q_full, i + 1)
                s.activation(QT[:, i * HALF:(i + 1) * HALF], PS[i][:, :], ACT.Identity, bias=BQ1[:, 0:1]).then_inc(q_ready, 1)
            attention(0, float(DK) ** -0.5)
            turned(3, split=True, affine=True)
            gate(1, RT[:, 0, :])
            mixture(1)
            turned(4)
            act.wait_ge(wq_full, 1)
            copy(W2Q[:, 0:I2], PS[0][:, 0:I2])
            copy(W2Q[:, I2:2 * I2], PS[1][:, 0:I2])
            for c in range(3):
                k = min(128, I2 - 128 * c)
                last = copy(W2Q[0:k, 2 * I2 + c * D:2 * I2 + (c + 1) * D], PS[2][0:k, c * D:(c + 1) * D])
            last.then_inc(wq_copied, 1)
            turned(5)
            for t in range(B):
                act.wait_ge(f2_up, t + 1)
                if t >= 2:
                    act.wait_ge(f2_q, t - 1)
                s.activation(HG[:, (t % 2) * I2:(t % 2 + 1) * I2], PS[2 * (t % 2)][:, 0:I2], ACT.Silu).then_inc(f2_silu, 1)
                act.wait_ge(f2_t, t + 1)
                copy(HQT[:, 3 * S * (t % 2):3 * S * (t % 2) + 2 * S], PS[4 + t % 2][:, 0:2 * S])
                copy(HQT[0:I2 - 256, 3 * S * (t % 2) + 2 * S:3 * S * (t % 2 + 1)],
                     PS[4 + t % 2][0:I2 - 256, 2 * S:3 * S]).then_inc(f2_tc, 1)
            turned(6)
            for i in range(2):
                act.wait_ge(k3_full, i + 1)
                copy(K3T[:, i * 4 * KC:(i + 1) * 4 * KC], PS[2 + i][:, 0:4 * KC]).then_inc(k3_ready, 1)
            for i in range(2):
                act.wait_ge(q_full, i + 3)
                copy(QT[:, i * HALF:(i + 1) * HALF], PS[i][:, :]).then_inc(q_ready, 1)
            for i in range(2):
                act.wait_ge(v3_full, i + 1)
                last = copy(V1[:, 4 * i:4 * i + 4, :].rearrange("k b (h d) -> k (b h) d", h=NH)[:, :, 0:DK],
                            PS[4 + i][0:KC, :].rearrange("k (n d) -> k n d", d=DK))
                last.then_inc(v3_ready, 1)
            attention(B, float(D) ** -0.5)
            for i in range(2):
                act.wait_ge(ont_full, i + 1)
                copy(ONT[:, i * HALF:(i + 1) * HALF], PS[i][:, :]).then_inc(ont_ready, 1)
            turned(7, split=True)
            gate(2, RT[:, 0, :])
            mixture(3)

        @block.vector
        def _(dve):
            v = nc.vector
            steps = [0]

            def step(ins):
                steps[0] += 1
                ins.then_inc(dve_step, 1)

            def settle():
                dve.wait_ge(dve_step, steps[0])

            def now(ins):
                step(ins)
                settle()

            def tg(i):
                return TG[:, i:i + 1]

            def norm(n, src, dst):
                for t in range(B):
                    step(v.bn_stats(ST[:, t, :], src[:, t, :]))
                settle()
                for t in range(B):
                    step(v.bn_aggr(MV[:, t, :], ST[:, t, :]))
                settle()
                v.tensor_scalar(VE[:, :], MV[:, :, 1], EPS, None, ALU.add).then_inc(var_ready, 1)
                dve.wait_ge(rstd_ready, n + 1)
                for t in range(B):
                    v.tensor_scalar(dst[:, t, :], src[:, t, :], MV[:, t, 0:1], RSTD[:, t:t + 1],
                                    ALU.subtract, ALU.mult).then_inc(xn_ready, 1)

            def low_of_xt(k, n):
                for h in range(2):
                    dve.wait_ge(xt_ready, 2 * k + h + 1)
                    c = slice(h * HALF, (h + 1) * HALF)
                    v.tensor_tensor(XTl[:, c], XT[:, c], XTh[:, c].bitcast(fp32), ALU.subtract).then_inc(xtl_ready, 1)

            def high_parts(u):
                dve.wait_ge(raw_loaded[u % 2], LOADED[u])
                if u >= 2:
                    dve.wait_ge(unit_used, u - 1)
                for p, c, n, _ in PARTS[u]:
                    last = v.tensor_copy(WH[0:p, u % 2, c:c + n], RAW[0:p, u % 2, c:c + n])
                last.then_inc(hi_done, 1)

            def per_token(m, row):
                return m[:, row, :].rearrange("p (t o) -> p t o", o=1).to_broadcast([128, B, E])

            def route(n, layer):
                rt = lambda i: RT[:, i, :]
                rt3 = lambda i: RT[:, i, :].rearrange("p (t e) -> p t e", e=E)
                rev = REV[:, :, :].rearrange("p t e -> p (t e)")
                dve.wait_ge(v1_ready, 1)
                dve.wait_ge(logit_full, n + 1)
                lg = PS[4][:, 0:B * E]
                if layer == 3:
                    now(v.tensor_tensor(rt3(9), lg.rearrange("p (t e) -> p t e", e=E),
                                        RB3[:, :].rearrange("p (o e) -> p o e", o=1).to_broadcast([128, B, E]), ALU.add))
                else:
                    now(v.tensor_copy(rt(9), lg))
                now(v.tensor_reduce(RM[:, 0, :], rt3(9), AX.X, ALU.max))
                v.tensor_tensor(rt3(0), rt3(9), per_token(RM, 0), ALU.subtract).then_inc(dif_ready, 1)
                dve.wait_ge(gate_exp, n + 1)
                if layer == 3:
                    scores, prob = 9, 1
                else:
                    now(v.tensor_reduce(RM[:, 1, :], rt3(1), AX.X, ALU.add))
                    now(v.reciprocal(RM[:, 2, :], RM[:, 1, :]))
                    now(v.tensor_tensor(rt3(2), rt3(1), per_token(RM, 2), ALU.mult))
                    scores = prob = 2
                for pick in range(2):
                    now(v.tensor_reduce(RM[:, 0, :], rt3(scores), AX.X, ALU.max))
                    now(v.tensor_tensor(rt3(3), rt3(scores), per_token(RM, 0), ALU.is_equal))
                    now(v.tensor_tensor(rt(4), rt(3), rev, ALU.mult))
                    now(v.tensor_reduce(RM[:, 0, :], rt3(4), AX.X, ALU.max))
                    now(v.tensor_tensor(rt3(5 + pick), rt3(4), per_token(RM, 0), ALU.is_equal))
                    if pick == 0:
                        now(v.scalar_tensor_tensor(rt(7), rt(5), -1.0e30, rt(scores), ALU.mult, ALU.add))
                        scores = 7
                now(v.tensor_tensor(rt(8), rt(5), rt(6), ALU.add))
                now(v.tensor_tensor(rt(8), rt(8), rt(prob), ALU.mult))
                now(v.tensor_reduce(RM[:, 0, :], rt3(8), AX.X, ALU.add))
                if layer == 0:
                    now(v.tensor_scalar(RM[:, 0, :], RM[:, 0, :], 1e-20, None, ALU.add))
                now(v.reciprocal(RM[:, 1, :], RM[:, 0, :]))
                now(v.tensor_tensor(rt3(8), rt3(8), per_token(RM, 1), ALU.mult))
                v.tensor_scalar(WG[:, n, :], rt(8), tg(4 + layer), None, ALU.mult).then_inc(wg_ready, 1)

            def mixture(n, layer, extra=None):
                dve.wait_ge(wg_ready, n + 1)
                for st in stages_of(layer):
                    kind, e, h = st["kind"], st["e"], st["h"]
                    if kind == "up" and layer == 0:
                        for c in range(2):
                            j, k = st["job"] + 2 * c + 1, st["hid"] + c
                            dve.wait_ge(act_freed, CONSUMERS[j - 1][1])
                            dve.wait_ge(ring_full, j + 1)
                            hc = slice(c * HALF, (c + 1) * HALF)
                            v.tensor_tensor(G[0:C0, k % 4, :], SG[0:C0, k % 4, :], PS[j % NRING][0:C0, :],
                                            ALU.mult).then_inc(dve_freed, 1)
                            dve.wait_ge(dve_freed, CONSUMERS[j][1])
                            now(v.tensor_copy(H1h[0:C0, h, hc], G[0:C0, k % 4, :]))
                            v.tensor_tensor(H1l[0:C0, h, hc], G[0:C0, k % 4, :], H1h[0:C0, h, hc].bitcast(fp32),
                                            ALU.subtract).then_inc(split_done, 1)
                    elif kind in ("up", "spec1a", "spec2", "turn"):
                        hi, lo = (H1h, H1l) if kind == "up" else (H2h, H2l)
                        for c in range(2 if kind == "spec1a" else 4):
                            j, k = st["job"] + c, st["hid"] + c
                            dve.wait_ge(act_freed, CONSUMERS[j][1])
                            hc = slice(c * HALF, (c + 1) * HALF)
                            v.tensor_tensor(lo[:, h, hc], G[:, k % 4, :], hi[:, h, hc].bitcast(fp32),
                                            ALU.subtract).then_inc(split_done, 1)
                    elif kind in ("spec0", "spec1b"):
                        def stats(t):
                            j = st["job"] + t
                            i = TH * h + t
                            dve.wait_ge(ring_full, j + 1)
                            now(v.bn_stats(ST[:, i, :], PS[j % NRING][:, :]))
                            now(v.bn_aggr(MV[:, i, :], ST[:, i, :]))
                            v.tensor_scalar(VE[:, i:i + 1], MV[:, i, 1:2], EPS, None, ALU.add).then_inc(tvar_ready, 1)

                        def scale(t):
                            j = st["job"] + t
                            i = TH * h + t
                            dve.wait_ge(trstd_ready, st["norm"] + t + 1)
                            v.tensor_scalar(SN[:, h, t * F1:(t + 1) * F1], PS[j % NRING][:, :], MV[:, i, 0:1],
                                            RSTD[:, i:i + 1], ALU.subtract, ALU.mult).then_inc(dve_freed, 1)

                        stats(0)
                        for t in range(1, TH):
                            stats(t)
                            scale(t - 1)
                        scale(TH - 1)
                    elif kind in ("down", "bias"):
                        d = st["down"]
                        dve.wait_ge(down_full, d + 1)
                        for t in range(TH):
                            i = TH * h + t
                            x = X[:, i, :]
                            y = PS[4 + d % 2][:, t * D:(t + 1) * D]
                            if kind == "bias":
                                last = v.tensor_tensor(x, y, x, ALU.add)
                            else:
                                w = WG[:, n, i * E + e:i * E + e + 1] if e < E else tg(4 + layer)
                                last = v.scalar_tensor_tensor(x, y, w, x, ALU.mult, ALU.add)
                        last.then_inc(down_free, 1)
                        dve.wait_ge(down_free, d + 1)
                        if kind == "down" and h == 1 and st["unit"] + 2 < NUNITS:
                            high_parts(st["unit"] + 2)
                            if extra and e == 2:
                                extra()

            def attention(first, layer):
                def scores(b):
                    for i, (h0, h1) in enumerate(HEADS):
                        dve.wait_ge(s_full, 3 * b + i + 1)
                        n = h1 - h0
                        step(v.tensor_reduce(MX[:, h0:h1], PS[i][:, 0:n * KC].rearrange("p (h k) -> p h k", h=n), AX.X, ALU.max))
                    settle()
                    if b > first:
                        dve.wait_ge(exp_done, b)
                    for i, (h0, h1) in enumerate(HEADS):
                        n = h1 - h0
                        last = v.tensor_tensor(SUB[:, h0 * KC:h1 * KC].rearrange("p (h k) -> p h k", h=n),
                                               PS[i][:, 0:n * KC].rearrange("p (h k) -> p h k", h=n),
                                               MX[:, h0:h1].rearrange("p (h o) -> p h o", o=1).to_broadcast([128, n, KC]),
                                               ALU.subtract)
                    last.then_inc(sub_done, 1)

                def weighted(b):
                    for i in range(2, 4):
                        dve.wait_ge(pt_full, 4 * b + i + 1)
                        v.tensor_copy(PT[:, i * HALF:(i + 1) * HALF], PS[3 + i][0:KC, :]).then_inc(pt_dve, 1)
                    dve.wait_ge(o_full, b + 1)
                    o = PS[7][:, 0:NH * (DK + 1)].rearrange("p (h d) -> p h d", h=NH)
                    now(v.reciprocal(RC[:, :], o[:, :, DK]))
                    t = b - first
                    rc = RC
                    if layer == 1:
                        now(v.tensor_scalar(RC2[:, :], RC[:, :], ANY[:, t:t + 1], None, ALU.mult))
                        rc = RC2
                        dst = TMP
                    else:
                        dst = ON[:, t * D:(t + 1) * D]
                    v.tensor_tensor(dst.rearrange("p (h d) -> p h d", h=NH), o[:, :, 0:DK],
                                    rc[:, :].rearrange("p (h o) -> p h o", o=1).to_broadcast([128, NH, DK]),
                                    ALU.mult).then_inc(o_done, 1)
                    dve.wait_ge(o_done, b + 1)
                    if layer == 1:
                        now(v.tensor_tensor(X[:, t, :], X[:, t, :], TMP, ALU.add))

                for b in range(first, first + B):
                    scores(b)
                    if b > first:
                        weighted(b - 1)
                weighted(first + B - 1)

            def quantise(src, dst, n, parts=128):
                nb = n // QB
                p = slice(0, parts)
                blk = lambda x: x.rearrange("p (b k) -> p b k", k=QB)
                per = lambda i: QS[p, i, 0:nb].rearrange("p (b o) -> p b o", o=1).to_broadcast([parts, nb, QB])
                now(v.tensor_reduce(QS[p, 0, 0:nb], blk(src), AX.X, ALU.max, apply_absolute_value=True))
                now(v.tensor_scalar(QS[p, 0, 0:nb], QS[p, 0, 0:nb], 1.0 / 6.0, 1e-12, ALU.mult, ALU.max))
                now(v.reciprocal(QS[p, 1, 0:nb], QS[p, 0, 0:nb]))
                step(v.tensor_scalar(QS[p, 2, 0:nb], QS[p, 0, 0:nb], 0.5, None, ALU.mult))
                m, q = QA[p, 0:n], QC[p, 0:n]
                now(v.tensor_tensor(blk(m), blk(src), per(1), ALU.mult))
                now(v.tensor_scalar(m.bitcast(u32), m.bitcast(u32), 0x7FFFFFFF, None, ALU.bitwise_and))
                now(v.tensor_scalar(q, m, 5.0, 2.0, ALU.is_gt, ALU.mult))
                for mid in (3.5, 2.5):
                    now(v.scalar_tensor_tensor(q, m, mid, q, ALU.is_gt, ALU.add))
                now(v.tensor_scalar(q, q, 2.0, None, ALU.mult))
                for mid in (1.75, 1.25, 0.75, 0.25):
                    now(v.scalar_tensor_tensor(q, m, mid, q, ALU.is_gt, ALU.add))
                now(v.tensor_tensor(blk(q), blk(q), per(2), ALU.mult))
                return v.scalar_tensor_tensor(dst.bitcast(u32), src.bitcast(u32), 0x80000000, q.bitcast(u32),
                                              ALU.bitwise_and, ALU.bitwise_or)

            dve.wait_ge(in_x, 16)
            for t in range(B):
                step(v.bn_stats(ST[:, t, :], X[:, t, :]))
            dve.wait_ge(pool_const, 6)
            v.tensor_copy(identb[:, :], ident[:, :]).then_inc(const_copied, 1)
            settle()
            norm(0, X, XN)
            dve.wait_ge(mask1_in, 16)
            now(v.tensor_scalar(SUB[:, 0:B * KC], MI[:, :], 0.0, None, ALU.not_equal))
            now(v.tensor_reduce(ANY[:, :], SUB[:, 0:B * KC].rearrange("p (b k) -> p b k", b=B), AX.X, ALU.max))
            dve.wait_ge(tg_ready, 1)
            now(v.tensor_scalar(ANY[:, :], ANY[:, :], tg(1), None, ALU.mult))
            v.tensor_scalar(MB1[:, :], MI[:, :], 0.0, MASKED, ALU.is_equal, ALU.mult).then_inc(const_copied, 1)
            dve.wait_ge(const_copied, 2)
            high_parts(0)
            dve.wait_ge(in_small, SMALL_IN)
            now(v.memset(ROWr[:, :].bitcast(fp32), 0.0))
            now(v.tensor_copy(ROWr[0:1, :], ROW[0:1, :]))
            now(v.tensor_copy(ROWr[32:33, :], ROW[32:33, :]))
            v.tensor_tensor(ROWr[32:33, :], ROW[32:33, :], ROWr[32:33, :].bitcast(fp32), ALU.subtract).then_inc(row_ready, 1)

            for i in range(2):
                dve.wait_ge(a0_s, i + 1)
                now(v.tensor_reduce(MX[:, 4 * i:4 * i + 4], PS[4 + i][:, 0:4 * KC].rearrange("p (b k) -> p b k", b=4), AX.X, ALU.max))
                v.tensor_tensor(SUB[:, i * 4 * KC:(i + 1) * 4 * KC].rearrange("p (b k) -> p b k", b=4),
                                PS[4 + i][:, 0:4 * KC].rearrange("p (b k) -> p b k", b=4),
                                MX[:, 4 * i:4 * i + 4].rearrange("p (b o) -> p b o", o=1).to_broadcast([128, 4, KC]),
                                ALU.subtract).then_inc(a0_sub, 1)
            dve.wait_ge(a0_exp, 2)
            now(v.tensor_reduce(RC[:, 0:B], PB[:, 0:B * KC].rearrange("p (b k) -> p b k", b=B), AX.X, ALU.add))
            now(v.reciprocal(RC[:, 8:8 + B], RC[:, 0:B]))
            now(v.tensor_scalar(RC[:, 0:B], RC[:, 8:8 + B], tg(0), None, ALU.mult))
            for i in range(2):
                dve.wait_ge(a0_o, i + 1)
                for t in range(TH):
                    b = TH * i + t
                    step(v.scalar_tensor_tensor(X[:, b, :], PS[i][:, t * D:(t + 1) * D], RC[:, b:b + 1], X[:, b, :],
                                                ALU.mult, ALU.add))
            settle()
            norm(1, X, XN)
            low_of_xt(1, 0)
            high_parts(1)
            route(0, 0)
            mixture(0, 0)
            norm(2, X, XN)
            attention(0, 1)
            norm(3, X, XN)
            dve.wait_ge(xn_ready, 4 * B)
            norm(4, XN, XM)
            now(v.scalar_tensor_tensor(X[:, :, :].rearrange("p b d -> p (b d)"), XN[:, :, :].rearrange("p b d -> p (b d)"),
                                       tg(5), X[:, :, :].rearrange("p b d -> p (b d)"), ALU.mult, ALU.add))
            low_of_xt(3, 1)
            route(1, 1)
            mixture(1, 1)
            norm(5, X, XN)
            now(v.tensor_reduce(CS[:, :], CT[:, :].rearrange("p (b k) -> p b k", b=B), AX.X, ALU.add))
            v.tensor_scalar(CSB.rearrange("p (b s) -> p b s", b=B),
                            CS[:, :].rearrange("p (b o) -> p b o", o=1).to_broadcast([128, B, S]), 1.0 / KC, None,
                            ALU.mult).then_inc(csb_ready, 1)
            dve.wait_ge(in_w2, 16 * len(LAYER2))
            for m in range(2):
                for c in range(3):
                    k = min(128, I2 - 128 * c)
                    now(quantise(W2R[0:k, m, c, :], W2R[0:k, m, c, :], D, k))
            wd = W2R[:, 2, :, :].rearrange("p c k -> p (c k)")[:, 0:I2]
            quantise(wd, wd, I2).then_inc(wq_ready, 1)
            dve.wait_ge(wq_ready, 1)
            for h in range(2):
                dve.wait_ge(a2_full, h + 1)
                xh = X[:, TH * h:TH * h + TH, :].rearrange("p b d -> p (b d)")
                now(v.scalar_tensor_tensor(xh, PS[4 + h][:, :], tg(2), xh, ALU.mult, ALU.add))
            norm(6, X, XN)
            dve.wait_ge(xn_ready, 7 * B)
            quantise(XN[:, :, :].rearrange("p b d -> p (b d)"), XQ, T).then_inc(xq_ready, 1)
            dve.wait_ge(xq_ready, 1)
            for t in range(B):
                dve.wait_ge(f2_silu, t + 1)
                hg = HG[:, (t % 2) * I2:(t % 2 + 1) * I2]
                v.tensor_tensor(QD[:, 0:I2], hg, PS[2 * (t % 2) + 1][:, 0:I2], ALU.mult).then_inc(f2_used, 1)
                dve.wait_ge(f2_used, t + 1)
                if t >= 2:
                    dve.wait_ge(f2_t, t - 1)
                quantise(QD[:, 0:I2], HQ[:, (t % 2) * I2:(t % 2 + 1) * I2], I2).then_inc(f2_q, 1)
                dve.wait_ge(f2_q, t + 1)
                if t >= 1:
                    dve.wait_ge(f2_down, t)
                    now(v.scalar_tensor_tensor(X[:, t - 1, :], PS[6 + (t - 1) % 2][:, 0:D], tg(6), X[:, t - 1, :],
                                               ALU.mult, ALU.add))
            dve.wait_ge(f2_down, B)
            now(v.scalar_tensor_tensor(X[:, B - 1, :], PS[6 + (B - 1) % 2][:, 0:D], tg(6), X[:, B - 1, :], ALU.mult, ALU.add))
            dve.wait_ge(mask3_in, 16)
            now(v.tensor_scalar(MB3[:, :], MI[:, :], 0.0, MASKED, ALU.is_equal, ALU.mult))
            for m in range(3):
                last = v.tensor_tensor(BD3[:, m, :].rearrange("p (h e) -> p h e", h=NH),
                                       WQK[:, m * DK:(m + 1) * DK].rearrange("p (o e) -> p o e", o=1).to_broadcast([128, NH, DK]),
                                       HM[:, :].rearrange("p (h o) -> p h o", o=1).to_broadcast([128, NH, DK]), ALU.mult)
            last.then_inc(bd3_ready, 1)
            norm(7, X, XN)
            attention(B, 3)
            for h in range(2):
                dve.wait_ge(wo_full, h + 1)
                xh = X[:, TH * h:TH * h + TH, :].rearrange("p b d -> p (b d)")
                now(v.scalar_tensor_tensor(xh, PS[2 + h][:, :], tg(3), xh, ALU.mult, ALU.add))
            norm(8, X, XN)
            low_of_xt(7, 2)
            route(2, 3)
            mixture(2, 3)

        @block.tensor
        def _(pe):
            t_ = nc.tensor

            def mm(o, l, r, start=True, stop=True):
                return t_.matmul(o, l, r, start=start, stop=stop)

            def mm3(o, l, r, start, stop):
                mm(o, l[0], r[0], start, False)
                mm(o, l[0], r[1], False, False)
                return mm(o, l[1], r[0], False, stop)

            def turn(k, src, ready):
                for h in range(2):
                    for t in range(TH):
                        i = TH * h + t
                        ready(i)
                        last = t_.transpose(PS[6 + h][:, t * S:(t + 1) * S], src(i), ident[:, :])
                    last.then_inc(xnt_full, 1)

            def normed(n, buf):
                return lambda i: buf[:, i, :], lambda i: pe.wait_ge(xn_ready, n * B + i + 1)

            def logits(n, w, k):
                for t in range(B):
                    if t % TH == 0:
                        pe.wait_ge(xt_ready, 2 * k + t // TH + 1)
                    last = mm(PS[4][:, t * E:(t + 1) * E], XT[:, t * S:(t + 1) * S], w)
                last.then_inc(logit_full, 1)

            def ring(j):
                if j >= NRING:
                    eng, n = CONSUMERS[j - NRING]
                    pe.wait_ge(act_freed if eng == "act" else dve_freed, n)
                return PS[j % NRING]

            def mixture(n, layer, first_xtl):
                for st in stages_of(layer):
                    kind, e, h, u = st["kind"], st["e"], st["h"], st["unit"]
                    w = (WH[:, u % 2, :], WL[:, u % 2, :])
                    j, k = st["job"], st["hid"]
                    x = (XTh[:, h * HALF:(h + 1) * HALF], XTl[:, h * HALF:(h + 1) * HALF])
                    h1, h2 = (H1h[:, h, :], H1l[:, h, :]), (H2h[:, h, :], H2l[:, h, :])

                    def cols(pair, c0, n, p=128):
                        return tuple(m[0:p, c0:c0 + n] for m in pair)

                    if kind == "up":
                        pe.wait_ge(lo_done, u + 1)
                        pe.wait_ge(xtl_ready, first_xtl + h + 1)
                        if layer == 0:
                            for c in range(2):
                                for m in range(2):
                                    o = ring(j + 2 * c + m)
                                    mm3(o[0:C0, :], cols(w, m * I0 + c * C0, C0), x, True, True).then_inc(ring_full, 1)
                        else:
                            for c in range(4):
                                mm3(ring(j + c)[:, :], cols(w, c * 128, 128), x, True, True).then_inc(ring_full, 1)
                    elif kind in ("spec1a", "spec2"):
                        nc_, width = (2, F2) if kind == "spec1a" else (4, F1)
                        up = next(s for s in STAGES if s["kind"] == "up" and s["unit"] == u and s["h"] == h)
                        pe.wait_ge(split_done, up["hid"] + 4)
                        for c in range(nc_):
                            o = ring(j + c)
                            for f in range(4):
                                last = mm3(o[:, :], cols(w, F1 + f * width + c * 128, 128), cols(h1, f * HALF, HALF),
                                           f == 0, f == 3)
                            last.then_inc(ring_full, 1)
                    elif kind in ("spec0", "spec1b"):
                        if kind == "spec0":
                            src = next(s for s in STAGES if s["kind"] == "up" and s["unit"] == u and s["h"] == h)
                            pe.wait_ge(split_done, src["hid"] + 4)
                            hh, nf, at, row = h1, 4, F1, e // 4
                        else:
                            src = next(s for s in STAGES if s["kind"] == "spec1a" and s["unit"] == u and s["h"] == h)
                            pe.wait_ge(split_done, src["hid"] + 2)
                            hh, nf, at, row = h2, 2, F1 + 4 * F2, 2 + e // 4
                        if u == 10:
                            pe.wait_ge(row_ready, 1)
                        for t in range(TH):
                            o = ring(j + t)
                            mm(o[:, :], onesr[:, :], ROWr[:, row * F1:(row + 1) * F1], True, False)
                            for f in range(nf):
                                last = mm3(o[:, :], cols(hh, f * HALF + t * S, S), cols(w, at + f * F1, F1), False, f == nf - 1)
                            last.then_inc(ring_full, 1)
                    elif kind == "turn":
                        src = next(s for s in STAGES if s["kind"] in ("spec0", "spec1b") and s["unit"] == u and s["h"] == h)
                        pe.wait_ge(dve_freed, src["dve"] + TH)
                        for c in range(4):
                            o = ring(j + c)
                            for t in range(TH):
                                last = t_.transpose(o[:, t * S:(t + 1) * S], SN[:, h, t * F1 + c * 128:t * F1 + (c + 1) * 128],
                                                    ident[:, :])
                            last.then_inc(ring_full, 1)
                    elif kind == "down":
                        src = [s for s in STAGES if s["kind"] in ("up", "spec2", "turn") and s["unit"] == u and s["h"] == h][-1]
                        nf = 2 if layer == 0 else 4
                        pe.wait_ge(split_done, src["hid"] + nf)
                        d = st["down"]
                        if d >= 2:
                            pe.wait_ge(down_free, d - 1)
                        if d < 2 or st["e"] == 0:
                            pe.wait_ge(wg_ready, n + 1)
                        hh = h1 if src["kind"] == "up" else h2
                        p, at = (C0 if layer == 0 else 128), down_at(u)
                        for t in range(TH):
                            for f in range(nf):
                                last = mm3(PS[4 + d % 2][:, t * D:(t + 1) * D], cols(hh, f * HALF + t * S, S, p),
                                           cols(w, at + f * D, D, p), f == 0, f == nf - 1)
                        last.then_inc(down_full, 1)
                        if h == 1:
                            pe.wait_ge(down_full, d + 1)
                            pe.sem_inc(unit_used, 1)
                    elif kind == "bias":
                        db = DB1 if layer == 1 else DB3
                        if h == 0:
                            for i in range(2):
                                for t in range(TH):
                                    b = TH * i + t
                                    last = mm(PS[6 + i][0:E, t * S:(t + 1) * S], WG[:, n, b * E:(b + 1) * E], ident[:, :])
                                last.then_inc(wgt_full, 1)
                        pe.wait_ge(wgt_ready, (0 if layer == 1 else 2) + h + 1)
                        d = st["down"]
                        pe.wait_ge(down_free, d - 1)
                        for t in range(TH):
                            b = TH * h + t
                            last = mm(PS[4 + d % 2][:, t * D:(t + 1) * D], WGT[:, b * S:(b + 1) * S], db[:, :])
                        last.then_inc(down_full, 1)

            def attention(first, mb):
                def scores(b):
                    pe.wait_ge(bdk_ready, b + 1)
                    if b > first:
                        pe.wait_ge(sub_done, b)
                    t = b - first
                    for i, (h0, h1) in enumerate(HEADS):
                        n = h1 - h0
                        o = PS[i][:, 0:n * KC]
                        mm(o, QT[:, t * S:(t + 1) * S], BDK[:, b % 2, h0 * KC:h1 * KC], True, False)
                        mask = mb[:, t * KC:(t + 1) * KC].rearrange("p (o k) -> p o k", o=1).to_broadcast([128, n, KC])
                        mm(o.rearrange("p (h k) -> p h k", h=n), identb[:, :], mask, False, True).then_inc(s_full, 1)

                scores(first)
                for b in range(first, first + B):
                    if b + 1 < first + B:
                        scores(b + 1)
                    t = b - first
                    pe.wait_ge(exp_done, b + 1)
                    for i in range(4):
                        if b > first:
                            if i < 2:
                                pe.wait_ge(pt_act, 2 * (b - 1) + i + 1)
                            else:
                                pe.wait_ge(pt_dve, 2 * (b - 1) + i - 1)
                        for m in range(4):
                            h = 4 * i + m
                            last = t_.transpose(PS[3 + i][0:KC, m * S:(m + 1) * S], PB[:, h * KC:(h + 1) * KC], ident[:, :])
                        last.then_inc(pt_full, 1)
                    pe.wait_ge(pt_act, 2 * b + 2)
                    pe.wait_ge(pt_dve, 2 * b + 2)
                    if b > first:
                        pe.wait_ge(o_done, b)
                    for h in range(NH):
                        c = slice(h * (DK + 1), (h + 1) * (DK + 1))
                        last = mm(PS[7][:, c], PT[:, h * S:(h + 1) * S], V1[:, t, c])
                    last.then_inc(o_full, 1)

            pe.wait_ge(pool_const, 6)
            pe.wait_ge(in_ctx, 16)
            for b in range(B):
                last = t_.transpose(PS[4 + b // 4][:, (b % 4) * KC:(b % 4 + 1) * KC], CTX[:, b, :], ident[0:KC, 0:KC])
                if b % 4 == 3:
                    last.then_inc(ctxt_full, 1)
            turn(0, *normed(0, XN))
            pe.wait_ge(in_small, SMALL_IN)
            for i in range(2):
                pe.wait_ge(xt_ready, i + 1)
                mm(PS[i][0:R0, :], Wu[:, :], XT[:, i * HALF:(i + 1) * HALF]).then_inc(a0_up, 1)
            for i in range(2):
                pe.wait_ge(ct_ready, i + 1)
                mm(PS[2 + i][0:R0, 0:4 * KC], Wv[:, :], CT[:, i * 4 * KC:(i + 1) * 4 * KC]).then_inc(a0_up, 1)
            pe.wait_ge(a0_upc, 4)
            for b in range(B):
                last = mm(PS[4 + b // 4][:, (b % 4) * KC:(b % 4 + 1) * KC], U0T[:, b * S:(b + 1) * S], VP0[:, b * KC:(b + 1) * KC])
                if b % 4 == 3:
                    last.then_inc(a0_s, 1)
            for b in range(B):
                pe.wait_ge(a0_exp, b // 4 + 1)
                last = t_.transpose(PS[6 + b // 4][0:KC, (b % 4) * S:(b % 4 + 1) * S], PB[:, b * KC:(b + 1) * KC], ident[:, :])
                if b % 4 == 3:
                    last.then_inc(a0_pt, 1)
            for b in range(B):
                pe.wait_ge(a0_ptc, b // 4 + 1)
                last = mm(PS[b // 4][:, (b % 4) * D:(b % 4 + 1) * D], PT[:, b * S:(b + 1) * S], CTX[:, b, :])
                if b % 4 == 3:
                    last.then_inc(a0_o, 1)
            turn(1, *normed(1, XN))
            logits(0, GW0[:, :], 1)
            mixture(0, 0, 0)
            turn(2, *normed(2, XN))
            for i in range(2):
                pe.wait_ge(xt_ready, 4 + i + 1)
                mm(PS[i][:, :], WQ1[:, :], XT[:, i * HALF:(i + 1) * HALF]).then_inc(q_full, 1)
            pe.wait_ge(v1_ready, 1)
            pe.wait_ge(q_ready, 2)
            attention(0, MB1)
            turn(3, *normed(4, XM))
            logits(1, RW1[:, :], 3)
            mixture(1, 1, 2)
            turn(4, *normed(5, XN))
            pe.wait_ge(csb_ready, 1)
            pe.wait_ge(in_w2, 16 * len(LAYER2))
            for t in range(B):
                if t % TH == 0:
                    pe.wait_ge(xt_ready, 8 + t // TH + 1)
                o = PS[4 + t // TH][:, (t % TH) * D:(t % TH + 1) * D]
                mm(o, XT[:, t * S:(t + 1) * S], W2A[:, 0:D], True, False)
                mm(o, CSB[:, t * S:(t + 1) * S], W2A[:, D:2 * D], False, False)
                last = mm(o, ones[:, :], B2A[:, :], False, True)
                if t % TH == TH - 1:
                    last.then_inc(a2_full, 1)
            pe.wait_ge(wq_ready, 1)
            for m in range(2):
                for c in range(3):
                    k = min(128, I2 - 128 * c)
                    t_.transpose(PS[m][:, c * 128:c * 128 + k], W2R[0:k, m, c, :], ident[0:k, 0:k])
            wd = W2R[:, 2, :, :].rearrange("p c k -> p (c k)")
            for c in range(3):
                k = min(128, I2 - 128 * c)
                last = t_.transpose(PS[2][0:k, c * D:(c + 1) * D], wd[:, c * 128:c * 128 + k], ident[:, :])
            last.then_inc(wq_full, 1)
            turn(5, lambda i: XQ[:, i * D:(i + 1) * D], lambda i: pe.wait_ge(xq_ready, 1))
            pe.wait_ge(wq_copied, 1)

            def down2(t):
                pe.wait_ge(f2_tc, t + 1)
                for c in range(3):
                    k = min(128, I2 - 128 * c)
                    at = 3 * S * (t % 2) + c * S
                    last = mm(PS[6 + t % 2][:, 0:D], HQT[0:k, at:at + S], W2Q[0:k, 2 * I2 + c * D:2 * I2 + (c + 1) * D], c == 0, c == 2)
                last.then_inc(f2_down, 1)

            def up2(t):
                if t % TH == 0:
                    pe.wait_ge(xt_ready, 10 + t // TH + 1)
                if t >= 2:
                    pe.wait_ge(f2_used, t - 1)
                mm(PS[2 * (t % 2)][:, 0:I2], XT[:, t * S:(t + 1) * S], W2Q[:, 0:I2])
                mm(PS[2 * (t % 2) + 1][:, 0:I2], XT[:, t * S:(t + 1) * S], W2Q[:, I2:2 * I2]).then_inc(f2_up, 1)

            up2(0)
            pe.wait_ge(xt_ready, 12)
            for t in range(B):
                if t + 1 < B:
                    up2(t + 1)
                pe.wait_ge(f2_q, t + 1)
                for c in range(3):
                    k = min(128, I2 - 128 * c)
                    last = t_.transpose(PS[4 + t % 2][0:k, c * S:(c + 1) * S],
                                        HQ[:, (t % 2) * I2 + c * 128:(t % 2) * I2 + c * 128 + k], ident[:, :])
                last.then_inc(f2_t, 1)
                down2(t)
            pe.wait_ge(bd3_ready, 1)
            for i in range(2):
                mm(PS[2 + i][:, 0:4 * KC], BD3[:, 1, :], CT[:, i * 4 * KC:(i + 1) * 4 * KC]).then_inc(k3_full, 1)
            for b in range(B):
                last = mm(PS[4 + b // 4][0:KC, (b % 4) * D:(b % 4 + 1) * D], CT[:, b * KC:(b + 1) * KC], BD3[:, 2, :])
                if b % 4 == 3:
                    last.then_inc(v3_full, 1)
            turn(6, *normed(7, XN))
            for i in range(2):
                pe.wait_ge(xt_ready, 12 + i + 1)
                mm(PS[i][:, :], BD3[:, 0, :], XT[:, i * HALF:(i + 1) * HALF]).then_inc(q_full, 1)
            pe.wait_ge(v3_ready, 2)
            pe.wait_ge(q_ready, 4)
            attention(B, MB3)
            pe.wait_ge(o_done, 2 * B)
            for b in range(B):
                last = t_.transpose(PS[b // 4][:, (b % 4) * S:(b % 4 + 1) * S], ON[:, b * D:(b + 1) * D], ident[:, :])
                if b % 4 == 3:
                    last.then_inc(ont_full, 1)
            for b in range(B):
                pe.wait_ge(ont_ready, b // 4 + 1)
                o = PS[2 + b // 4][:, (b % 4) * D:(b % 4 + 1) * D]
                mm(o, ONT[:, b * S:(b + 1) * S], WO3[:, :], True, False)
                last = mm(o, ones[:, :], BO3[:, :], False, True)
                if b % 4 == 3:
                    last.then_inc(wo_full, 1)
            turn(7, *normed(8, XN))
            logits(2, RW3[:, :], 7)
            mixture(2, 3, 4)


HEADS = [(0, 6), (6, 12), (12, 16)]


def layouts(x):
    c = np.ascontiguousarray
    cols = lambda m: c(np.moveaxis(m.reshape(m.shape[0], -1, 128), 2, 0).reshape(128, -1))
    own = ["x", "ctx_1024", "mask_Bx1xS2_ik0", "mask_Bx1xSxS2_ik1", "g_xattn", "g_ffn", "L0_xattn_Wu", "L0_xattn_Wv",
           "L0_ffn_wg", "L0_ffn_wu", "L0_ffn_wd", "L0_ffn_swg", "L0_ffn_swu", "L0_ffn_swd",
           "L1_ffn_router_w", "L1_ffn_up_W", "L1_ffn_down_W", "L1_ffn_down_b", "L1_ffn_spec0_W", "L1_ffn_spec1a_W",
           "L1_ffn_spec1b_W", "L1_ffn_spec2_W", "L2_ffn_w_gate", "L2_ffn_w_up", "L2_ffn_w_down",
           "L3_ffn_router_w", "L3_ffn_router_b", "L3_ffn_w1", "L3_ffn_w2", "L3_ffn_b2"]
    r = {n: c(x[n]) for n in own}
    r["L0_gate_T"] = c(x["L0_ffn_gate_w"].T)
    r["L1_Wq_T"] = c(x["L1_xattn_Wq"].T)
    r["L1_bq_col"] = c(x["L1_xattn_bq"].reshape(128, 1))
    r["L1_ln_g_col"] = c(x["L1_ffn_ln_g"].reshape(128, 1))
    r["L1_ln_b_col"] = c(x["L1_ffn_ln_b"].reshape(128, 1))
    for n in ("up_b", "spec1a_b", "spec2_b", "ln0_g", "ln0_b", "ln1_g", "ln1_b"):
        r[f"L1_{n}_cols"] = cols(x[f"L1_ffn_{n}"])
    r["L1_spec0_b_row"] = c(x["L1_ffn_spec0_b"].reshape(1, -1))
    r["L1_spec1b_b_row"] = c(x["L1_ffn_spec1b_b"].reshape(1, -1))
    w = x["L2_xattn_W"]
    r["L2_W_T"] = c(np.concatenate([w[:, 0:D].T, w[:, D:].T], axis=1))
    r["L2_b_row"] = c(x["L2_xattn_b"].reshape(1, -1))
    r["L3_WqkvT_heads"] = c(np.tile(np.concatenate([x[f"L3_xattn_W{k}"].T for k in "qkv"], axis=1), (NH, 1)))
    r["L3_Wo_T"] = c(x["L3_xattn_Wo"].T)
    r["L3_bo_row"] = c(x["L3_xattn_bo"].reshape(1, -1))
    r["L3_b1_cols"] = cols(x["L3_ffn_b1"])
    return r


def kernel(**inputs):
    import concourse.bacc as bacc
    from concourse.bass_utils import run_bass_kernel_spmd

    nc = bacc.Bacc("TRN2", target_bir_lowering=False, num_devices=1)
    arrays, handles = {}, {}
    for name, m in layouts({k: np.asarray(v) for k, v in inputs.items()}).items():
        arrays[f"in_{name}"] = m
        handles[name] = nc.dram_tensor(f"in_{name}", m.shape, mybir.dt.from_np(m.dtype), kind="ExternalInput").ap()
    out = nc.dram_tensor("out", (B, S, D), mybir.dt.float32, kind="ExternalOutput").ap()
    program(nc, handles, out)
    r = run_bass_kernel_spmd(nc, [arrays], core_ids=[0])
    return r.results[0]["out"]
```

```python
import numpy as np
import concourse.bass as bass
from concourse import mybir
from contextlib import ExitStack

B, S, D = 8, 128, 128
T = B * S
KC = 77
NH, DK = 16, 8
R0 = 32
E = 8
HALF = 512
TH = HALF // S
I0 = 176
F1, F2 = 512, 256
F3 = 512
I2 = 352
QB = 16
EPS = 1e-5
MASKED = -1.0e30
RAWCOLS, WCOLS = 3072, 6144
E0P = 5
U0COLS = 4 * I0 + 3 * D
RING = (0, 1, 2, 3, 6, 7)


def weave(*lists):
    out = []
    for n in range(max(len(x) + i for i, x in enumerate(lists))):
        for i, x in enumerate(lists):
            if 0 <= n - i < len(x):
                out.append(x[n - i])
    return out


def plan():
    areas = []
    at = dict(raw=0)

    def area(unit, kind, base, cols, rows=128):
        raw = at["raw"] if at["raw"] + cols <= RAWCOLS else 0
        at["raw"] = raw + cols
        areas.append(dict(unit=unit, kind=kind, base=base, cols=cols, rows=rows, raw=raw, n=len(areas)))

    for p in range(E0P):
        b = p * U0COLS
        area(p, "gate", b, 2 * I0)
        area(p, "up", b + 2 * I0, 2 * I0)
        area(p, "down", b + 4 * I0, 2 * D)
        area(p, "down_rest", b + 4 * I0 + 2 * D, D, 2 * I0 - 256)
    low, mid = (0, 4096), (1024, 2048)
    place = [low, mid, low, (1024, None), (0, 2048), (1024, 4096), (0, 2048), (1024, None)]
    for e in range(E):
        ud, inner = place[e]
        u = E0P + e
        area(u, "up", ud, F1)
        if inner is not None:
            area(u, "inner", inner, 4 * F1)
        area(u, "down", ud + F1, 4 * D)
    for e in range(E):
        u = E0P + E + e
        area(u, "up", (e % 6) * 1024, F3)
        area(u, "down", (e % 6) * 1024 + F3, 4 * D)

    def piece(kind, layer, e, h, i, **more):
        unit = {0: 0, 1: E0P, 3: E0P + E}[layer] + e
        return dict(kind=kind, layer=layer, e=e, h=h, i=i, unit=unit, **more)

    def strips(unit, kinds=None):
        out = []
        for a in areas:
            if a["unit"] == unit and (kinds is None or a["kind"] in kinds):
                n = -(-a["cols"] // HALF)
                for k in range(n):
                    c0, c1 = a["cols"] * k // n, a["cols"] * (k + 1) // n
                    out.append(dict(kind="split", layer=None, unit=unit, area=a, c0=c0, c1=c1, last=k == n - 1))
        return out

    def group(kind, layer, e, h, n, **more):
        return [piece(kind, layer, e, h, i, **more) for i in range(n)]

    order = {0: [dict(kind="route")], 1: [], 3: []}
    before = {0: strips(0) + strips(1), 1: strips(E0P), 3: strips(E0P + E) + strips(E0P + E + 1)}
    x = [(p, h) for p in range(E0P) for h in range(2)]
    for n in range(len(x) + 2):
        a = group("gate_up", 0, *x[n], TH) if n < len(x) else []
        b = group("turn0", 0, *x[n - 1], 3, buf=(n - 1) % 4) if 1 <= n <= len(x) else []
        c = group("down0", 0, *x[n - 2], 3, buf=(n - 2) % 4) if n >= 2 else []
        more = strips(n // 2 + 2) if n % 2 == 0 and n // 2 + 2 < E0P else []
        order[0] += weave(a, b, c, more)
    def down_of(layer, e, h, buf):
        g = group("down", layer, e, h, 4, buf=buf)
        first = [piece("wgt", layer, e, k, 0) for k in range(2)] if e == 0 and h == 0 else []
        return g[:3] + first + [piece("spread", layer, e, h, 0)] + g[3:]

    up = lambda e, h: group("up", 1, e, h, 4, buf=h + (2 if e % 4 == 3 else 0), hi="act")
    down = lambda e, h: down_of(1, e, h, h + 2)
    o = order[1]
    o += up(0, 0)
    wq = [dict(kind="quantise", layer=1, i=i) for i in range(7)]
    for e in range(E):
        spec = lambda kind, h, n, **m: group(kind, 1, e, h, n, **m)
        nxt = up(e + 1, 0) if e + 1 < E else []
        if e + 1 >= E:
            new = []
        elif e % 4 == 2:
            new = strips(E0P + e + 1)
        elif e % 4 == 3:
            new = strips(E0P + e + 1, ("up", "down"))
        else:
            new = strips(E0P + e + 1)
        if e % 4 == 2 and e + 2 < E:
            new = new + strips(E0P + e + 2, ("inner",))
        q = []
        if e in (4, 5, 6):
            q, wq = wq[:3], wq[3:]
        if e % 4 == 0:
            o += weave(spec("spec0", 0, TH), up(e, 1), new[:4])
            if e == 0:
                o.append(dict(kind="route"))
            o += weave(spec("spec0", 1, TH), spec("turn", 0, 4, buf=2, hi="act"), new[4:], q)
            o += weave(spec("turn", 1, 4, buf=3, hi="act"), down(e, 0))
            o += weave(nxt, down(e, 1))
        elif e % 4 == 1:
            o += weave(spec("spec1a", 0, 2, buf=2, hi="act"), up(e, 1), new[:3])
            o += weave(spec("spec1a", 1, 2, buf=3, hi="act"), new[3:])
            o += weave(spec("spec1b", 0, TH), q)
            o += weave(spec("spec1b", 1, TH), spec("turn", 0, 4, buf=2, hi="act"))
            o += weave(spec("turn", 1, 4, buf=3, hi="act"), down(e, 0))
            o += weave(nxt, down(e, 1))
        elif e % 4 == 2:
            o += weave(spec("spec2", 0, 4, buf=2, hi="act"), up(e, 1), new[:2])
            o += weave(spec("spec2", 1, 4, buf=3, hi="act"), down(e, 0), new[2:], q)
            o += weave(nxt, down(e, 1))
        else:
            o += weave(up(e, 1), new)
            o += weave(nxt, down(e, 0))
            o += down(e, 1)
    x = [(e, h) for e in range(E) for h in range(2)]
    for n in range(len(x) + 2):
        a = group("up", 3, *x[n], 4, buf=n % 4) if n < len(x) else []
        for m in a:
            m["hi"] = "act" if m["i"] % 2 == 0 else "dve"
        c = down_of(3, *x[n - 2], (n - 2) % 4) if n >= 2 else []
        more = strips(E0P + E + n // 2 + 2) if n % 2 == 0 and n // 2 + 2 < E else []
        order[3] += weave(a, c, more)
        if n == 1:
            order[3].append(dict(kind="route"))

    n = dict(job=0, act=0, dve=0, hid=0, down=0, norm=0, strip=0, add=0)
    readers, slot_free = [], []
    for layer in (0, 1, 3):
        for s in before[layer] + order[layer]:
            k = s["kind"]
            s["job"] = n["job"]
            if k == "split":
                n["strip"] += 1
                s["strip"] = n["strip"]
                s["area"]["ready"] = n["strip"]
                if "first" not in s["area"]:
                    s["area"]["first"] = n["strip"]
            elif k == "gate_up":
                n["act"] += 1
                n["dve"] += 1
                readers += [("act", n["act"]), ("dve", n["dve"])]
            elif k == "turn0":
                n["hid"] += 1
                readers.append(("split", n["hid"]))
            elif k in ("up", "spec1a", "spec2", "turn"):
                n["act"] += 1
                n["hid"] += 1
                readers.append(("act", n["act"]))
                s["g"] = len(slot_free)
                slot_free.append(n["hid"])
            elif k in ("spec0", "spec1b"):
                n["dve"] += 1
                n["norm"] += 1
                readers.append(("dve", n["dve"]))
            elif k in ("wgt", "spread"):
                n["act"] += 1
                readers.append(("act", n["act"]))
            elif k == "down" and s["i"] == 3:
                n["down"] += 1
                n["add"] += s["e"] > 0
            n["job"] = len(readers)
            s.update({c: n[c] for c in ("act", "dve", "hid", "down", "norm", "add")})
    for a in areas:
        over = [b for b in areas[:a["n"]] if b["base"] < a["base"] + a["cols"] and a["base"] < b["base"] + b["cols"]]
        a["after_unit"] = max([b["unit"] for b in over if b["unit"] != a["unit"]], default=None)
        over = [b for b in areas[:a["n"]] if b["raw"] < a["raw"] + a["cols"] and a["raw"] < b["raw"] + b["cols"]]
        a["after_strip"] = max([b["ready"] for b in over], default=0)
    return before, order, readers, slot_free, areas


def program(nc, a, out):
    fp32, fp32r = mybir.dt.float32, mybir.dt.float32r
    bf16, i32, u32 = mybir.dt.bfloat16, mybir.dt.int32, mybir.dt.uint32
    ALU, ACT, AX = mybir.AluOpType, mybir.ActivationFunctionType, mybir.AxisListType
    BEFORE, ORDER, READERS, SLOT_FREE, AREAS = plan()
    NRING = len(RING)
    LAST0, LAST1, LAST3 = ORDER[0][-1], ORDER[1][-1], ORDER[3][-1]

    def group(ring, g):
        return ring[:, (g % 3) * GH * KC:(g % 3 + 1) * GH * KC]

    def area_source(r):
        u, kind = r["unit"], r["kind"]
        if u < E0P:
            if kind in ("gate", "up"):
                if u < E0P - 1:
                    w = a["L0_ffn_wg" if kind == "gate" else "L0_ffn_wu"]
                    return w[2 * u:2 * u + 2].rearrange("e p i -> p e i")
                return a["L0_ffn_swg" if kind == "gate" else "L0_ffn_swu"]
            d = a["L0_ffn_swd"] if u == E0P - 1 else a["L0_ffn_wd"][2 * u:2 * u + 2].rearrange("e i h -> (e i) h")
            return d[0:256].rearrange("(c p) h -> p c h", p=128) if kind == "down" else d[256:2 * I0]
        layer, e = (1, u - E0P) if u < E0P + E else (3, u - E0P - E)
        if kind == "up":
            return a["L1_ffn_up_W" if layer == 1 else "L3_ffn_w1"][e]
        if kind == "down":
            return a["L1_ffn_down_W" if layer == 1 else "L3_ffn_w2"][e].rearrange("(c p) h -> p c h", p=128)
        if e % 4 == 1:
            return None
        return a["L1_ffn_spec0_W" if e % 4 == 0 else "L1_ffn_spec2_W"][e // 4].rearrange("(c p) f -> p c f", p=128)

    def area_loads(r):
        if r["unit"] >= E0P and r["kind"] == "inner" and (r["unit"] - E0P) % 4 == 1:
            g = (r["unit"] - E0P) // 4
            return [(0, 4 * F2, a["L1_ffn_spec1a_W"][g].rearrange("(c p) f -> p c f", p=128)),
                    (4 * F2, 2 * F1, a["L1_ffn_spec1b_W"][g].rearrange("(c p) f -> p c f", p=128))]
        return [(0, r["cols"], area_source(r))]

    def area_of(unit, kind):
        return next(r for r in AREAS if r["unit"] == unit and r["kind"] == kind)

    def hidden_ready(unit, h, kinds, i):
        return max(s["hid"] for layer in ORDER for s in ORDER[layer]
                   if s["kind"] in kinds and s["unit"] == unit and s["h"] == h and s["i"] == i)

    ctx = ExitStack()
    with ctx:
        def sb(name, shape, dt=fp32):
            return ctx.enter_context(nc.sbuf_tensor(name, shape, dt))

        def sem(name):
            return ctx.enter_context(nc.semaphore(name))

        X = sb("X", [128, B, D])
        XN = sb("XN", [128, B, D])
        XT = sb("XT", [128, T])
        XTh = sb("XTh", [128, T], fp32r)
        XTl = sb("XTl", [128, T], fp32r)
        ctx_at = nc.sbuf_base
        CTX = sb("CTX", [KC, B, D])
        CT = sb("CT", [128, B * KC])
        V1 = sb("V1", [KC, B, NH * (DK + 1)])
        RAW = sb("RAW", [128, RAWCOLS])
        WH = sb("WH", [128, WCOLS], fp32r)
        WL = sb("WL", [128, WCOLS], fp32r)
        hidden_at = nc.sbuf_base
        hidden_bytes = 2 * 4 * HALF * 4
        H1h = sb("H1h", [128, 2, 4 * HALF], fp32r)
        H1l = sb("H1l", [128, 2, 4 * HALF], fp32r)
        H2h = sb("H2h", [128, 2, 4 * HALF], fp32r)
        H2l = sb("H2l", [128, 2, 4 * HALF], fp32r)

        def over(name, i, shape):
            return nc.alloc_sbuf_tensor_at(name, shape, fp32, offset=hidden_at + i * hidden_bytes)

        G = sb("G", [128, 4, HALF])
        turned_at = nc.sbuf_base
        SN = sb("SN", [128, 2, 4 * HALF])
        XM = nc.alloc_sbuf_tensor_at("XM", [128, B, D], fp32, offset=turned_at)
        WGS = nc.alloc_sbuf_tensor_at("WGS", [128, B, 3 * 32], bf16, offset=ctx_at + 4 * 10 * B * E)
        WGT = sb("WGT", [3 * 32, T], bf16)
        PICK = sb("PICK", [3 * 32, E], bf16)
        BDK = nc.alloc_sbuf_tensor_at("BDK", [128, 2, NH * KC], fp32, offset=turned_at)
        HID = [(H1h[:, 0, :], H1l[:, 0, :]), (H1h[:, 1, :], H1l[:, 1, :]),
               (H2h[:, 0, :], H2l[:, 0, :]), (H2h[:, 1, :], H2l[:, 1, :])]
        ATT = over("ATT", 0, [128, 8 * HALF])
        ATT3 = over("ATT3", 1, [128, 8 * HALF])
        ATT2 = over("ATT2", 2, [128, 8 * HALF])
        QT = ATT[:, 0:T]
        SUB = ATT[:, 1024:1024 + NH * KC]
        PB = ATT[:, 2304:2304 + NH * KC]
        PT = ATT2[0:KC, 0:NH * S]
        ON = ATT2[:, 2048:3072]
        TMP = ATT3[:, 0:D]
        ONT = ATT3[:, 1024:2048]
        K3T = ATT3[:, 2048:2048 + B * KC]
        U0T = ATT[0:R0, 0:T]
        VP0 = ATT3[0:R0, 0:B * KC]
        CSB = ATT2[:, 0:T]
        QA = ATT[:, 0:T]
        QC = ATT[:, 1024:2048]
        QD = ATT[:, 2048:3072]
        XQ = ATT2[:, 0:T]
        HG = ATT2[:, 1024:1024 + 2 * I2]
        HQ = ATT2[:, 2048:2048 + 2 * I2]
        HQT = ATT3[:, 0:2 * 3 * S]
        ident = sb("ident", [128, 128])
        identb = sb("identb", [128, 128], bf16)
        ones = sb("ones", [1, 128])
        onesr = sb("onesr", [33, 128], fp32r)
        HM = sb("HM", [128, NH])
        REV = sb("REV", [128, B, E])
        TG = sb("TG", [128, 8])
        GB = sb("GB", [128, 8])
        Wu = sb("Wu", [128, R0])
        Wv = sb("Wv", [128, R0])
        GW0 = sb("GW0", [128, E])
        WQ1 = sb("WQ1", [128, D])
        BQ1 = sb("BQ1", [128, 1])
        LNG = sb("LNG", [128, 2])
        RW1 = sb("RW1", [128, E])
        UB1 = sb("UB1", [128, 4 * E])
        SB1 = sb("SB1", [128, 2 * (2 + 4)])
        LG1 = sb("LG1", [128, 4 * 4])
        LB1 = sb("LB1", [128, 4 * 4])
        ROW = over("ROW", 3, [33, 4 * F1])
        ROWr = sb("ROWr", [33, 4 * F1], fp32r)
        DB1 = sb("DB1", [128, E])
        W2A = sb("W2A", [128, 2 * D])
        B2A = sb("B2A", [1, D])
        W2R = sb("W2R", [128, 3, 3, D])
        W2S = [sb("W2S0", [128, I2]), sb("W2S1", [128, I2])]
        W2Q = over("W2Q", 3, [128, 2 * I2 + 3 * D])
        WQK = sb("WQK", [128, 3 * DK])
        BD3 = nc.alloc_sbuf_tensor_at("BD3", [128, 3, D], fp32, offset=hidden_at + 2 * hidden_bytes + 4 * 3072)
        WO3 = sb("WO3", [128, D])
        BO3 = sb("BO3", [1, D])
        RW3 = sb("RW3", [128, E])
        RB3 = sb("RB3", [128, E])
        FB3 = sb("FB3", [128, 4 * E])
        DB3 = sb("DB3", [128, E])
        MI = nc.alloc_sbuf_tensor_at("MI", [128, B * KC], i32, offset=hidden_at + hidden_bytes + 4 * 2752)
        MB1 = sb("MB1", [128, B * KC], bf16)
        MB3 = nc.alloc_sbuf_tensor_at("MB3", [128, B * KC], bf16, offset=ctx_at + 4 * 10 * B * E)
        ANY = sb("ANY", [128, B])
        CS = sb("CS", [128, B])
        ST = sb("ST", [128, B, 6])
        MV = sb("MV", [128, B, 2])
        VE = sb("VE", [128, B])
        RSTD = sb("RSTD", [128, B])
        MHALF = sb("MHALF", [128, B])
        MX = sb("MX", [128, NH])
        RC = sb("RC", [128, NH])
        RC2 = sb("RC2", [128, NH])
        RT = nc.alloc_sbuf_tensor_at("RT", [128, 10, B * E], fp32, offset=ctx_at)
        WB = XN[:, :, :].rearrange("p b d -> p (b d)")
        YW = nc.alloc_sbuf_tensor_at("YW", [128, T], fp32, offset=ctx_at)
        RM = sb("RM", [128, 4, B])
        WG = sb("WG", [128, B * E])
        QS = sb("QS", [128, 2, 64])

        PS = [ctx.enter_context(nc.psum_tensor(f"PS{i}", [128, HALF], fp32)) for i in range(8)]

        in_x, in_ctx, in_small = sem("in_x"), sem("in_ctx"), sem("in_small")
        in_w2 = sem("in_w2")
        mask1_in, mask3_in = sem("mask1_in"), sem("mask3_in")
        loaded = [sem(f"loaded{r['n']}") for r in AREAS]
        pool_const, pool_step = sem("pool_const"), sem("pool_step")
        dve_step, act_step = sem("dve_step"), sem("act_step")
        const_copied = sem("const_copied")
        var_ready, rstd_ready, xn_ready = sem("var_ready"), sem("rstd_ready"), sem("xn_ready")
        xnt_full, xt_ready, xtl_ready = sem("xnt_full"), sem("xt_ready"), sem("xtl_ready")
        ctxt_full, ct_ready = sem("ctxt_full"), sem("ct_ready")
        tg_ready = sem("tg_ready")
        a0_up, a0_upc, a0_s, a0_sub, a0_exp = sem("a0_up"), sem("a0_upc"), sem("a0_s"), sem("a0_sub"), sem("a0_exp")
        a0_pt, a0_ptc, a0_o = sem("a0_pt"), sem("a0_ptc"), sem("a0_o")
        q_full, q_ready = sem("q_full"), sem("q_ready")
        v1_ready, k3_full, k3_ready, v3_full, v3_ready = (sem("v1_ready"), sem("k3_full"), sem("k3_ready"),
                                                          sem("v3_full"), sem("v3_ready"))
        bd3_ready = sem("bd3_ready")
        bdk_ready, s_full, sub_done, exp_done = sem("bdk_ready"), sem("s_full"), sem("sub_done"), sem("exp_done")
        pt_full, pt_act, pt_dve, o_full, o_done = sem("pt_full"), sem("pt_act"), sem("pt_dve"), sem("o_full"), sem("o_done")
        ont_full, ont_ready, wo_full = sem("ont_full"), sem("ont_ready"), sem("wo_full")
        max_done = sem("max_done")
        csb_ready, a2_full = sem("csb_ready"), sem("a2_full")
        logit_full, dif_ready, gate_exp = sem("logit_full"), sem("dif_ready"), sem("gate_exp")
        wg_ready, wgs_ready = sem("wg_ready"), sem("wgs_ready")
        hi_done, lo_done = sem("hi_done"), sem("lo_done")
        y0_full, y0_copied, y_turned = sem("y0_full"), sem("y0_copied"), sem("y_turned")
        y_added, x_done = sem("y_added"), sem("x_done")
        act_high = sem("act_high")
        ring_full, act_freed, dve_freed = sem("ring_full"), sem("act_freed"), sem("dve_freed")
        split_done, down_full, down_free = sem("split_done"), sem("down_full"), sem("down_free")
        tvar_ready, trstd_ready, norm_done = sem("tvar_ready"), sem("trstd_ready"), sem("norm_done")
        wq_ready, wq_full, wq_copied, xq_ready = sem("wq_ready"), sem("wq_full"), sem("wq_copied"), sem("xq_ready")
        f2_up, f2_silu, f2_q, f2_t, f2_tc, f2_down = (sem("f2_up"), sem("f2_silu"), sem("f2_q"), sem("f2_t"),
                                                      sem("f2_tc"), sem("f2_down"))
        f2_used = sem("f2_used")
        row_ready = sem("row_ready")
        stored = sem("stored")

        def copied_out(g):
            return (pt_dve, g // NG + 1) if g % NG == NG - 1 else (pt_act, (NG - 1) * (g // NG) + g % NG + 1)

        def unit_used(eng, unit):
            if unit < E0P:
                eng.wait_ge(y0_full, 2)
            else:
                eng.wait_ge(down_full, max(s["down"] for layer in (1, 3) for s in ORDER[layer]
                                           if s["kind"] == "down" and s["unit"] == unit))

        def reader(j):
            name, n = READERS[j]
            return {"act": act_freed, "dve": dve_freed, "split": split_done}[name], n

        def weights(r, c0, c1, rows=None):
            rows = r["rows"] if rows is None else rows
            return WH[0:rows, r["base"] + c0:r["base"] + c1], WL[0:rows, r["base"] + c0:r["base"] + c1]

        SMALL = [
            (Wu[:, :], a["L0_xattn_Wu"]), (Wv[:, :], a["L0_xattn_Wv"]),
            (GB[:, 0:4], a["g_xattn"].partition_broadcast(128)),
            (GB[:, 4:8], a["g_ffn"].partition_broadcast(128)),
            (GW0[:, :], a["L0_gate_T"]), (WQ1[:, :], a["L1_Wq_T"]), (BQ1[:, :], a["L1_bq_col"]),
            (LNG[:, 0:1], a["L1_ln_g_col"]), (LNG[:, 1:2], a["L1_ln_b_col"]),
            (RW1[:, :], a["L1_ffn_router_w"]), (UB1[:, :], a["L1_up_b_cols"]),
            (SB1[:, 0:4], a["L1_spec1a_b_cols"]), (SB1[:, 4:12], a["L1_spec2_b_cols"]),
            (LG1[:, 0:8], a["L1_ln0_g_cols"]), (LG1[:, 8:16], a["L1_ln1_g_cols"]),
            (LB1[:, 0:8], a["L1_ln0_b_cols"]), (LB1[:, 8:16], a["L1_ln1_b_cols"]),
            (DB1[:, :], a["L1_down_b_T"]), (B2A[:, :], a["L2_b_row"]),
            (WQK[:, :], a["L3_WqkvT_heads"]), (WO3[:, :], a["L3_Wo_T"]), (BO3[:, :], a["L3_bo_row"]),
            (RW3[:, :], a["L3_ffn_router_w"]), (RB3[:, :], a["L3_ffn_router_b"].partition_broadcast(128)),
            (FB3[:, :], a["L3_b1_cols"]), (DB3[:, :], a["L3_b2_T"]),
        ]
        for p in (0, 32):
            SMALL.append((ROW[p:p + 1, 0:2 * F1], a["L1_spec0_b_row"]))
            SMALL.append((ROW[p:p + 1, 2 * F1:4 * F1], a["L1_spec1b_b_row"]))
        LAYER2 = [(W2A[:, :], a["L2_W_T"])]
        for m, name in enumerate(("L2_ffn_w_gate", "L2_ffn_w_up")):
            for c in range(3):
                k = min(128, I2 - 128 * c)
                LAYER2.append((W2R[0:k, m, c, :], a[name][128 * c:128 * c + k, :]))
        LAYER2.append((W2R[:, 2, :, :].rearrange("p c k -> p (c k)")[:, 0:I2], a["L2_ffn_w_down"]))
        SMALL_IN = 16 * len(SMALL)

        block = ctx.enter_context(nc.Block())

        @block.sync
        def _(sp):
            sp.dma_start(X[:, :, :], a["x"].rearrange("b p d -> p b d")).then_inc(in_x, 16)
            sp.dma_start(CTX[:, :, :], a["ctx_1024"].rearrange("b k d -> k b d")).then_inc(in_ctx, 16)
            sp.dma_start(MI[:, :], a["mask_Bx1xS2_ik0"].rearrange("b o k -> (b o k)")
                         .partition_broadcast(128)).then_inc(mask1_in, 16)
            for r in AREAS:
                if r["after_strip"]:
                    sp.wait_ge(lo_done, r["after_strip"])
                for c, n, src in area_loads(r):
                    dst = RAW[0:r["rows"], r["raw"] + c:r["raw"] + c + n]
                    if len(src.shape) == 3:
                        dst = dst.rearrange("p (c n) -> p c n", c=src.shape[1])
                    sp.dma_start(dst, src).then_inc(loaded[r["n"]], 16)
                if r["unit"] == E0P and r["kind"] == "up":
                    for dst, src in LAYER2:
                        sp.dma_start(dst, src).then_inc(in_w2, 16)
                if r["unit"] == E0P + E + 1 and r["kind"] == "down":
                    sp.wait_ge(down_full, LAST1["down"])
                    sp.dma_start(MI[:, :].rearrange("q (b k) -> q b k", b=B),
                                 a["mask_Bx1xSxS2_ik1"].rearrange("b o q k -> q (b o) k")).then_inc(mask3_in, 16)
            for h in range(2):
                sp.wait_ge(x_done, h + 1)
                sp.dma_start(out[TH * h:TH * h + TH].rearrange("b p d -> p b d"),
                             X[:, TH * h:TH * h + TH, :]).then_inc(stored, 16)
            sp.wait_ge(stored, 32)

        @block.gpsimd
        def _(pool):
            steps = [0]

            def step(ins):
                steps[0] += 1
                ins.then_inc(pool_step, 1)
                pool.wait_ge(pool_step, steps[0])

            g = nc.gpsimd
            step(g.memset(ident[:, :], 0.0))
            g.affine_select(out=ident[:, :], in_=ident[:, :], compare_op=ALU.not_equal, fill=1.0, base=0,
                            pattern=[[-1, 128]], channel_multiplier=1).then_inc(pool_const, 1)
            g.memset(ones[:, :], 1.0).then_inc(pool_const, 1)
            g.memset(onesr[:, :].bitcast(fp32), 1.0).then_inc(pool_const, 1)
            step(g.memset(HM[:, :], 1.0))
            step(g.affine_select(out=HM[:, :], in_=HM[:, :], compare_op=ALU.is_ge, fill=0.0, base=0,
                                 pattern=[[-DK, NH]], channel_multiplier=1))
            g.affine_select(out=HM[:, :], in_=HM[:, :], compare_op=ALU.is_ge, fill=0.0, base=DK - 1,
                            pattern=[[DK, NH]], channel_multiplier=-1).then_inc(pool_const, 1)
            g.memset(MHALF[:, :], -0.5).then_inc(pool_const, 1)
            for e in range(E):
                last = g.memset(REV[:, :, e:e + 1], float(E - e))
            last.then_inc(pool_const, 1)
            pool.wait_ge(pool_const, 6)

            def rstd(n):
                pool.wait_ge(var_ready, n + 1)
                g.tensor_tensor(RSTD[:, :], VE[:, :], MHALF[:, :], ALU.pow).then_inc(rstd_ready, 1)

            def low_part(s):
                r = s["area"]
                pool.wait_ge(hi_done, s["strip"])
                hi, lo = weights(r, s["c0"], s["c1"])
                g.tensor_tensor(lo, RAW[0:r["rows"], r["raw"] + s["c0"]:r["raw"] + s["c1"]], hi.bitcast(fp32),
                                ALU.subtract).then_inc(lo_done, 1)

            def mixture(layer):
                for s in ORDER[layer]:
                    if s["kind"] == "split":
                        low_part(s)
                    elif s["kind"] in ("spec0", "spec1b"):
                        i = TH * s["h"] + s["i"]
                        pool.wait_ge(tvar_ready, s["norm"])
                        g.tensor_tensor(RSTD[:, i:i + 1], VE[:, i:i + 1], MHALF[:, 0:1], ALU.pow).then_inc(trstd_ready, 1)
                    elif s["kind"] == "down" and s["i"] == 3 and s["e"] > 0:
                        d = s["down"]
                        pool.wait_ge(down_free, d)
                        y = XT[:, s["h"] * HALF:(s["h"] + 1) * HALF]
                        if s["add"] > 1:
                            pool.wait_ge(y_added, s["add"] - 1)
                        g.tensor_tensor(y, y, YW[:, (d % 2) * HALF:(d % 2 + 1) * HALF], ALU.add).then_inc(y_added, 1)

            def prepare(layer):
                for s in BEFORE[layer]:
                    low_part(s)

            def head_keys(layer, kt):
                first = 0 if layer == 1 else B
                for b in range(first, first + B):
                    if b >= 2:
                        pool.wait_ge(s_full, NG * (b - 1))
                    keys = kt[:, (b - first) * KC:(b - first + 1) * KC].rearrange("p (o k) -> p o k", o=1)
                    heads = HM[:, :].rearrange("p (h o) -> p h o", o=1)
                    g.tensor_tensor(BDK[:, b % 2, :].rearrange("p (h k) -> p h k", h=NH),
                                    keys.to_broadcast([128, NH, KC]), heads.to_broadcast([128, NH, KC]),
                                    ALU.mult).then_inc(bdk_ready, 1)

            rstd(0)
            step(g.memset(PICK[:, :], 0.0))
            for k in range(3):
                step(g.affine_select(out=PICK[:, :], in_=PICK[:, :], compare_op=ALU.not_equal, fill=1.0,
                                     base=-32 * k, pattern=[[-1, E]], channel_multiplier=1))
            prepare(0)
            pool.wait_ge(in_ctx, 16)
            step(g.memset(V1[:, :, :], 1.0))
            g.tensor_copy(V1[:, :, :].rearrange("k b (h d) -> k b h d", h=NH)[:, :, :, 0:DK],
                          CTX[:, :, :].rearrange("k b (h d) -> k b h d", h=NH)).then_inc(v1_ready, 1)
            rstd(1)
            mixture(0)
            rstd(2)
            prepare(1)
            pool.wait_ge(ct_ready, 2)
            head_keys(1, CT)
            rstd(3)
            rstd(4)
            mixture(1)
            rstd(5)
            prepare(3)
            rstd(6)
            rstd(7)
            pool.wait_ge(k3_ready, 2)
            head_keys(3, K3T)
            rstd(8)
            mixture(3)

        @block.scalar
        def _(act):
            s = nc.scalar
            for dst, src in SMALL:
                act.dma_start(dst, src).then_inc(in_small, 16)

            def copy(o, i):
                return s.activation(o, i, ACT.Copy)

            def turned(k, split=False, affine=False):
                for h in range(2):
                    act.wait_ge(xnt_full, 2 * k + h + 1)
                    c = slice(h * HALF, (h + 1) * HALF)
                    dsts = [XT[:, c]] + ([XTh[:, c]] if split else [])
                    for d in dsts:
                        if affine:
                            last = s.activation(d, PS[6 + h][:, :], ACT.Identity, scale=LNG[:, 0:1], bias=LNG[:, 1:2])
                        else:
                            last = copy(d, PS[6 + h][:, :])
                    last.then_inc(xt_ready, 1)

            def mixture(n, layer):
                for s_ in ORDER[layer]:
                    kind = s_["kind"]
                    if kind in ("split", "quantise", "down", "down0", "spec0", "spec1b"):
                        continue
                    if kind == "route":
                        gate(n)
                        continue
                    e, h, i, j = s_["e"], s_["h"], s_["i"], s_["job"]
                    bank = PS[RING[j % NRING]]
                    if kind == "wgt":
                        act.wait_ge(ring_full, j + 1)
                        copy(WGT[:, h * HALF:(h + 1) * HALF], bank[0:96, :]).then_inc(act_freed, 1)
                    elif kind == "spread":
                        act.wait_ge(ring_full, j + 1)
                        d = s_["down"] + 1
                        if d > 2:
                            act.wait_ge(down_free, d - 2)
                        copy(WB[:, (d % 2) * HALF:(d % 2 + 1) * HALF], bank[:, :]).then_inc(act_freed, 1)
                    elif kind == "gate_up":
                        act.wait_ge(ring_full, j + 1)
                        k = s_["dve"] - 1
                        if k >= 4:
                            act.wait_ge(dve_freed, k - 3)
                        s.activation(G[:, k % 4, 0:2 * I0], bank[:, 0:2 * I0], ACT.Silu).then_inc(act_freed, 1)
                    elif kind == "turn0":
                        act.wait_ge(ring_full, j + 1)
                        rows = 128 if i < 2 else 2 * I0 - 256
                        copy(HID[s_["buf"]][0][0:rows, i * HALF:(i + 1) * HALF], bank[0:rows, :]).then_inc(act_high, 1)
                    else:
                        act.wait_ge(ring_full, j + 1)
                        k = s_["g"]
                        if k >= 4:
                            act.wait_ge(split_done, SLOT_FREE[k - 4])
                        scale = 1.0
                        if layer == 3:
                            func, bias = ACT.Relu, FB3[:, 4 * e + i:4 * e + i + 1]
                        elif kind == "up":
                            func, bias = ACT.Gelu, UB1[:, 4 * e + i:4 * e + i + 1]
                        elif kind == "spec1a":
                            func, bias = ACT.Gelu, SB1[:, 2 * (e // 4) + i:2 * (e // 4) + i + 1]
                        elif kind == "spec2":
                            func, bias = ACT.Gelu, SB1[:, 4 + 4 * (e // 4) + i:5 + 4 * (e // 4) + i]
                        else:
                            at = 8 * (e % 4) + 4 * (e // 4) + i
                            func = ACT.Gelu if e % 4 == 0 else ACT.Identity
                            scale, bias = LG1[:, at:at + 1], LB1[:, at:at + 1]
                        last = s.activation(G[:, k % 4, :], bank[:, :], func, bias=bias, scale=scale)
                        if s_["hi"] == "act":
                            last = s.activation(HID[s_["buf"]][0][:, i * HALF:(i + 1) * HALF], bank[:, :], func,
                                                bias=bias, scale=scale)
                        last.then_inc(act_freed, 1)

            def attention(first, scale):
                g0 = first * NG
                for i in range(B * NG + EVAC_LAG):
                    g = g0 + i - EVAC_LAG
                    if g >= g0 and g % NG != NG - 1:
                        act.wait_ge(pt_full, g + 1)
                        copy(PT[:, (g % 3) * HALF:(g % 3 + 1) * HALF], PS[3 + g % 3][0:KC, :]).then_inc(pt_act, 1)
                    g = g0 + i
                    if i < B * NG:
                        act.wait_ge(sub_done, g + 1)
                        if i >= 3:
                            act.wait_ge(pt_full, g - 2)
                        s.activation(group(PB, g), group(SUB, g), ACT.Exp, scale=scale).then_inc(exp_done, 1)

            act.wait_ge(in_small, SMALL_IN)
            s.activation(TG[:, :], GB[:, :], ACT.Tanh).then_inc(tg_ready, 1)
            for i in range(2):
                act.wait_ge(ctxt_full, i + 1)
                copy(CT[:, i * 4 * KC:(i + 1) * 4 * KC], PS[4 + i][:, 0:4 * KC]).then_inc(ct_ready, 1)
            turned(0)
            for i in range(2):
                act.wait_ge(a0_up, i + 1)
                copy(U0T[:, i * HALF:(i + 1) * HALF], PS[i][0:R0, :]).then_inc(a0_upc, 1)
            for i in range(2):
                act.wait_ge(a0_up, i + 3)
                copy(VP0[:, i * 4 * KC:(i + 1) * 4 * KC], PS[2 + i][0:R0, 0:4 * KC]).then_inc(a0_upc, 1)
            for i in range(2):
                act.wait_ge(a0_sub, i + 1)
                c = slice(i * 4 * KC, (i + 1) * 4 * KC)
                s.activation(PB[:, c], SUB[:, c], ACT.Exp, scale=float(R0) ** -0.5).then_inc(a0_exp, 1)
            for i in range(2):
                act.wait_ge(a0_pt, i + 1)
                copy(PT[:, i * HALF:(i + 1) * HALF], PS[6 + i][0:KC, :]).then_inc(a0_ptc, 1)

            def gate(n):
                act.wait_ge(dif_ready, n + 1)
                s.activation(RT[:, 1, :], RT[:, 0, :], ACT.Exp).then_inc(gate_exp, 1)

            turned(1, split=True)
            mixture(0, 0)
            for i in range(2):
                act.wait_ge(y0_full, i + 1)
                copy(XT[:, i * HALF:(i + 1) * HALF], PS[4 + i][:, :]).then_inc(y0_copied, 1)
            turned(2)
            for i in range(2):
                act.wait_ge(q_full, i + 1)
                s.activation(QT[:, i * HALF:(i + 1) * HALF], PS[i][:, :], ACT.Identity, bias=BQ1[:, 0:1]).then_inc(q_ready, 1)
            attention(0, float(DK) ** -0.5)
            turned(3, split=True, affine=True)
            mixture(1, 1)
            turned(4)
            act.wait_ge(wq_full, 1)
            copy(W2Q[:, 0:I2], PS[0][:, 0:I2])
            copy(W2Q[:, I2:2 * I2], PS[1][:, 0:I2])
            for c in range(3):
                k = min(128, I2 - 128 * c)
                last = copy(W2Q[0:k, 2 * I2 + c * D:2 * I2 + (c + 1) * D], PS[2][0:k, c * D:(c + 1) * D])
            last.then_inc(wq_copied, 1)
            turned(5)
            for t in range(B):
                act.wait_ge(f2_up, t + 1)
                if t >= 2:
                    act.wait_ge(f2_q, t - 1)
                s.activation(HG[:, (t % 2) * I2:(t % 2 + 1) * I2], PS[2 * (t % 2)][:, 0:I2], ACT.Silu).then_inc(f2_silu, 1)
                act.wait_ge(f2_t, t + 1)
                copy(HQT[:, 3 * S * (t % 2):3 * S * (t % 2) + 2 * S], PS[4 + t % 2][:, 0:2 * S])
                copy(HQT[0:I2 - 256, 3 * S * (t % 2) + 2 * S:3 * S * (t % 2 + 1)],
                     PS[4 + t % 2][0:I2 - 256, 2 * S:3 * S]).then_inc(f2_tc, 1)
            turned(6)
            for i in range(2):
                act.wait_ge(k3_full, i + 1)
                copy(K3T[:, i * 4 * KC:(i + 1) * 4 * KC], PS[2 + i][:, 0:4 * KC]).then_inc(k3_ready, 1)
            for i in range(2):
                act.wait_ge(q_full, i + 3)
                copy(QT[:, i * HALF:(i + 1) * HALF], PS[i][:, :]).then_inc(q_ready, 1)
            for i in range(2):
                act.wait_ge(v3_full, i + 1)
                last = copy(V1[:, 4 * i:4 * i + 4, :].rearrange("k b (h d) -> k (b h) d", h=NH)[:, :, 0:DK],
                            PS[4 + i][0:KC, :].rearrange("k (n d) -> k n d", d=DK))
                last.then_inc(v3_ready, 1)
            attention(B, float(D) ** -0.5)
            for i in range(2):
                act.wait_ge(ont_full, i + 1)
                copy(ONT[:, i * HALF:(i + 1) * HALF], PS[i][:, :]).then_inc(ont_ready, 1)
            turned(7, split=True)
            mixture(2, 3)

        @block.vector
        def _(dve):
            v = nc.vector
            steps = [0]

            def step(ins):
                steps[0] += 1
                ins.then_inc(dve_step, 1)

            def settle():
                dve.wait_ge(dve_step, steps[0])

            def now(ins):
                step(ins)
                settle()

            def tg(i):
                return TG[:, i:i + 1]

            def norm(n, src, dst):
                for t in range(B):
                    step(v.bn_stats(ST[:, t, :], src[:, t, :]))
                settle()
                for t in range(B):
                    step(v.bn_aggr(MV[:, t, :], ST[:, t, :]))
                settle()
                v.tensor_scalar(VE[:, :], MV[:, :, 1], EPS, None, ALU.add).then_inc(var_ready, 1)
                dve.wait_ge(rstd_ready, n + 1)
                for t in range(B):
                    v.tensor_scalar(dst[:, t, :], src[:, t, :], MV[:, t, 0:1], RSTD[:, t:t + 1],
                                    ALU.subtract, ALU.mult).then_inc(xn_ready, 1)

            def low_of_xt(k, n):
                for h in range(2):
                    dve.wait_ge(xt_ready, 2 * k + h + 1)
                    c = slice(h * HALF, (h + 1) * HALF)
                    v.tensor_tensor(XTl[:, c], XT[:, c], XTh[:, c].bitcast(fp32), ALU.subtract).then_inc(xtl_ready, 1)

            def high_part(s):
                r = s["area"]
                if s["strip"] == r["first"]:
                    dve.wait_ge(loaded[r["n"]], 16 * len(area_loads(r)))
                    if r["after_unit"] is not None:
                        unit_used(dve, r["after_unit"])
                hi, _ = weights(r, s["c0"], s["c1"])
                v.tensor_copy(hi, RAW[0:r["rows"], r["raw"] + s["c0"]:r["raw"] + s["c1"]]).then_inc(hi_done, 1)

            def prepare(layer):
                for s in BEFORE[layer]:
                    high_part(s)

            def per_token(m, row):
                return m[:, row, :].rearrange("p (t o) -> p t o", o=1).to_broadcast([128, B, E])

            def route(n, layer):
                rt = lambda i: RT[:, i, :]
                rt3 = lambda i: RT[:, i, :].rearrange("p (t e) -> p t e", e=E)
                rev = REV[:, :, :].rearrange("p t e -> p (t e)")
                dve.wait_ge(v1_ready, 1)
                dve.wait_ge(logit_full, n + 1)
                lg = PS[4][:, 0:B * E]
                if layer == 3:
                    now(v.tensor_tensor(rt3(9), lg.rearrange("p (t e) -> p t e", e=E),
                                        RB3[:, :].rearrange("p (o e) -> p o e", o=1).to_broadcast([128, B, E]), ALU.add))
                else:
                    now(v.tensor_copy(rt(9), lg))
                now(v.tensor_reduce(RM[:, 0, :], rt3(9), AX.X, ALU.max))
                v.tensor_tensor(rt3(0), rt3(9), per_token(RM, 0), ALU.subtract).then_inc(dif_ready, 1)
                dve.wait_ge(gate_exp, n + 1)
                if layer == 3:
                    scores, prob = 9, 1
                else:
                    now(v.tensor_reduce(RM[:, 1, :], rt3(1), AX.X, ALU.add))
                    now(v.reciprocal(RM[:, 2, :], RM[:, 1, :]))
                    now(v.tensor_tensor(rt3(2), rt3(1), per_token(RM, 2), ALU.mult))
                    scores = prob = 2
                for pick in range(2):
                    now(v.tensor_reduce(RM[:, 0, :], rt3(scores), AX.X, ALU.max))
                    now(v.tensor_tensor(rt3(3), rt3(scores), per_token(RM, 0), ALU.is_equal))
                    now(v.tensor_tensor(rt(4), rt(3), rev, ALU.mult))
                    now(v.tensor_reduce(RM[:, 0, :], rt3(4), AX.X, ALU.max))
                    now(v.tensor_tensor(rt3(5 + pick), rt3(4), per_token(RM, 0), ALU.is_equal))
                    if pick == 0:
                        now(v.scalar_tensor_tensor(rt(7), rt(5), -1.0e30, rt(scores), ALU.mult, ALU.add))
                        scores = 7
                now(v.tensor_tensor(rt(8), rt(5), rt(6), ALU.add))
                now(v.tensor_tensor(rt(8), rt(8), rt(prob), ALU.mult))
                now(v.tensor_reduce(RM[:, 0, :], rt3(8), AX.X, ALU.add))
                if layer == 0:
                    now(v.tensor_scalar(RM[:, 0, :], RM[:, 0, :], 1e-20, None, ALU.add))
                now(v.reciprocal(RM[:, 1, :], RM[:, 0, :]))
                now(v.tensor_tensor(rt3(8), rt3(8), per_token(RM, 1), ALU.mult))
                v.tensor_scalar(WG[:, :], rt(8), tg(4 + layer), None, ALU.mult).then_inc(wg_ready, 1)
                dve.wait_ge(wg_ready, n + 1)
                if layer > 0:
                    part = lambda k: WGS[:, :, 32 * k:32 * k + E]
                    wg = WG[:, :].rearrange("p (t e) -> p t e", e=E)
                    now(v.memset(WGS[:, :, :], 0.0))
                    now(v.tensor_copy(part(0), wg))
                    now(v.tensor_tensor(rt3(8), wg, part(0), ALU.subtract))
                    now(v.tensor_copy(part(1), rt3(8)))
                    v.tensor_tensor(part(2), rt3(8), part(1), ALU.subtract).then_inc(wgs_ready, 1)

            def mixture(n, layer):
                late = []
                owed = []

                def weigh(s):
                    d, h, e = s["down"], s["h"], s["e"]
                    dve.wait_ge(down_full, d)
                    dve.wait_ge(act_freed, s["act"])
                    at = slice((d % 2) * HALF, (d % 2 + 1) * HALF)
                    if e == 0:
                        dst = XT[:, h * HALF:(h + 1) * HALF]
                    else:
                        dst = YW[:, at]
                        if s["add"] > 2:
                            dve.wait_ge(y_added, s["add"] - 2)
                    db = DB1 if layer == 1 else DB3
                    v.scalar_tensor_tensor(dst, PS[4 + d % 2][:, :], db[:, e:e + 1], WB[:, at],
                                           ALU.add, ALU.mult).then_inc(down_free, 1)

                def tile_stats(s):
                    i = TH * s["h"] + s["i"]
                    bank = PS[RING[s["job"] % NRING]]
                    dve.wait_ge(ring_full, s["job"] + 1)
                    now(v.bn_stats(ST[:, i, :], bank[:, :]))
                    now(v.bn_aggr(MV[:, i, :], ST[:, i, :]))
                    v.tensor_scalar(VE[:, i:i + 1], MV[:, i, 1:2], EPS, None, ALU.add).then_inc(tvar_ready, 1)

                def tile_scale(s):
                    i = TH * s["h"] + s["i"]
                    bank = PS[RING[s["job"] % NRING]]
                    dve.wait_ge(trstd_ready, s["norm"])
                    v.tensor_scalar(SN[:, s["h"], s["i"] * F1:(s["i"] + 1) * F1], bank[:, :], MV[:, i, 0:1],
                                    RSTD[:, i:i + 1], ALU.subtract, ALU.mult).then_inc(dve_freed, 1)

                for s in ORDER[layer]:
                    kind, i, j = s["kind"], s.get("i"), s["job"]
                    h, e = s.get("h"), s.get("e")
                    ready, late = late, []
                    if owed and s["job"] >= owed[0]["job"] + WEIGH_JOBS:
                        weigh(owed.pop(0))
                    if kind == "split":
                        high_part(s)
                    elif kind == "route":
                        route(n, layer)
                    elif kind == "quantise":
                        quantise_weights(i)
                    elif kind == "gate_up":
                        bank = PS[RING[(j + 1) % NRING]]
                        k = s["dve"] - 1
                        dve.wait_ge(act_freed, s["act"])
                        dve.wait_ge(ring_full, j + 2)
                        t = TH * h + i
                        for m in range(2):
                            x = 2 * e + m
                            w = WG[:, t * E + x:t * E + x + 1] if x < E else tg(4)
                            c = slice(m * I0, (m + 1) * I0)
                            last = v.scalar_tensor_tensor(SN[:, h, i * 2 * I0 + m * I0:i * 2 * I0 + (m + 1) * I0],
                                                          bank[:, c], w, G[:, k % 4, c], ALU.mult, ALU.mult)
                        last.then_inc(dve_freed, 1)
                    elif kind == "turn0":
                        bank = PS[RING[j % NRING]]
                        rows = 128 if i < 2 else 2 * I0 - 256
                        hi, lo = (m[0:rows, i * HALF:(i + 1) * HALF] for m in HID[s["buf"]])
                        dve.wait_ge(act_high, s["hid"])
                        v.tensor_tensor(lo, bank[0:rows, :], hi.bitcast(fp32), ALU.subtract).then_inc(split_done, 1)
                    elif kind in ("up", "spec1a", "spec2", "turn"):
                        hi, lo = (m[:, i * HALF:(i + 1) * HALF] for m in HID[s["buf"]])
                        full = G[:, s["g"] % 4, :]
                        dve.wait_ge(act_freed, s["act"])
                        if s["hi"] == "dve":
                            now(v.tensor_copy(hi, full))
                        v.tensor_tensor(lo, full, hi.bitcast(fp32), ALU.subtract).then_inc(split_done, 1)
                    elif kind in ("spec0", "spec1b"):
                        tile_stats(s)
                        late = [s]
                        if i == TH - 1:
                            for m in ready:
                                tile_scale(m)
                            ready, late = [s], []
                    elif kind == "down" and i == 3:
                        owed.append(s)
                    for m in ready:
                        tile_scale(m)
                for s in owed:
                    weigh(s)

            def summed(n, last=False):
                for h in range(2):
                    dve.wait_ge(y_turned, 2 * n + h + 1)
                    xh = X[:, TH * h:TH * h + TH, :].rearrange("p b d -> p (b d)")
                    v.tensor_tensor(xh, PS[6 + h][:, :], xh, ALU.add).then_inc(x_done if last else dve_step, 1)
                    if not last:
                        steps[0] += 1
                settle()

            def attention(first, layer):
                g0 = first * NG

                def bank(g):
                    return PS[g % 3][:, 0:GH * KC].rearrange("p (h k) -> p h k", h=GH)

                def peak(g):
                    dve.wait_ge(s_full, g + 1)
                    v.tensor_reduce(MX[:, (g % 4) * GH:(g % 4 + 1) * GH], bank(g), AX.X, ALU.max).then_inc(max_done, 1)

                def below(g):
                    dve.wait_ge(max_done, g + 1)
                    if g - g0 >= 3:
                        dve.wait_ge(exp_done, g - 2)
                    top = MX[:, (g % 4) * GH:(g % 4 + 1) * GH].rearrange("p (h o) -> p h o", o=1)
                    v.tensor_tensor(group(SUB, g).rearrange("p (h k) -> p h k", h=GH), bank(g),
                                    top.to_broadcast([128, GH, KC]), ALU.subtract).then_inc(sub_done, 1)

                def evacuate(g):
                    dve.wait_ge(pt_full, g + 1)
                    v.tensor_copy(PT[:, (g % 3) * HALF:(g % 3 + 1) * HALF], PS[3 + g % 3][0:KC, :]).then_inc(pt_dve, 1)

                def weighted(b):
                    dve.wait_ge(o_full, b + 1)
                    o = PS[6 + b % 2][:, 0:NH * (DK + 1)].rearrange("p (h d) -> p h d", h=NH)
                    now(v.reciprocal(RC[:, :], o[:, :, DK]))
                    t = b - first
                    rc = RC
                    if layer == 1:
                        now(v.tensor_scalar(RC2[:, :], RC[:, :], ANY[:, t:t + 1], None, ALU.mult))
                        rc = RC2
                        dst = TMP
                    else:
                        dst = ON[:, t * D:(t + 1) * D]
                    v.tensor_tensor(dst.rearrange("p (h d) -> p h d", h=NH), o[:, :, 0:DK],
                                    rc[:, :].rearrange("p (h o) -> p h o", o=1).to_broadcast([128, NH, DK]),
                                    ALU.mult).then_inc(o_done, 1)
                    if layer == 1:
                        dve.wait_ge(o_done, b + 1)
                        step(v.tensor_tensor(X[:, t, :], X[:, t, :], TMP, ALU.add))

                for i in range(B * NG + WEIGH_LAG):
                    if i < B * NG:
                        peak(g0 + i)
                    g = g0 + i - 1
                    if g0 <= g < g0 + B * NG:
                        below(g)
                    g = g0 + i - TURN_LAG
                    if g0 <= g < g0 + B * NG and g % NG == NG - 1:
                        evacuate(g)
                    g = g0 + i - WEIGH_LAG + 1
                    if g >= g0 and g % NG == NG - 1:
                        weighted(g // NG)
                settle()

            def quantise(src, dst, n, parts=128, scratch=None):
                nb = n // QB
                p = slice(0, parts)
                blk = lambda x: x.rearrange("p (b k) -> p b k", k=QB)
                per = lambda i: QS[p, i, 0:nb].rearrange("p (b o) -> p b o", o=1).to_broadcast([parts, nb, QB])
                now(v.tensor_reduce(QS[p, 0, 0:nb], blk(src), AX.X, ALU.max, apply_absolute_value=True))
                now(v.tensor_scalar(QS[p, 0, 0:nb], QS[p, 0, 0:nb], 1.0 / 6.0, 1e-12, ALU.mult, ALU.max))
                now(v.reciprocal(QS[p, 1, 0:nb], QS[p, 0, 0:nb]))
                now(v.tensor_scalar(QS[p, 1, 0:nb], QS[p, 1, 0:nb], 1.0 - 2.0 ** -23, None, ALU.mult))
                m, q = (x[p, 0:n] for x in (scratch or (QA, QC)))
                now(v.tensor_tensor(blk(m), blk(src), per(1), ALU.mult))
                now(v.tensor_scalar(m.bitcast(u32), m.bitcast(u32), 0x7FFFFFFF, None, ALU.bitwise_and))
                now(v.tensor_scalar(q, m, 1.0, None, ALU.max))
                now(v.tensor_scalar(q.bitcast(u32), q.bitcast(u32), 0x7F800000, None, ALU.bitwise_and))
                now(v.scalar_tensor_tensor(m, q, 1.5 * 2.0 ** 22, m, ALU.mult, ALU.add))
                now(v.scalar_tensor_tensor(q, q, -1.5 * 2.0 ** 22, m, ALU.mult, ALU.add))
                now(v.tensor_tensor(blk(q), blk(q), per(0), ALU.mult))
                return v.scalar_tensor_tensor(dst.bitcast(u32), src.bitcast(u32), 0x80000000, q.bitcast(u32),
                                              ALU.bitwise_and, ALU.bitwise_or)

            def quantise_weights(i):
                if i == 0:
                    dve.wait_ge(in_w2, 16 * len(LAYER2))
                if i < 6:
                    k = min(128, I2 - 128 * (i % 3))
                    w = W2R[0:k, i // 3, i % 3, :]
                    now(quantise(w, w, D, k, W2S))
                else:
                    w = W2R[:, 2, :, :].rearrange("p c k -> p (c k)")[:, 0:I2]
                    quantise(w, w, I2, 128, W2S).then_inc(wq_ready, 1)
                    dve.wait_ge(wq_ready, 1)

            dve.wait_ge(in_x, 16)
            for t in range(B):
                step(v.bn_stats(ST[:, t, :], X[:, t, :]))
            dve.wait_ge(pool_const, 6)
            v.tensor_copy(identb[:, :], ident[:, :]).then_inc(const_copied, 1)
            settle()
            norm(0, X, XN)
            dve.wait_ge(mask1_in, 16)
            now(v.tensor_scalar(SUB[:, 0:B * KC], MI[:, :], 0.0, None, ALU.not_equal))
            now(v.tensor_reduce(ANY[:, :], SUB[:, 0:B * KC].rearrange("p (b k) -> p b k", b=B), AX.X, ALU.max))
            dve.wait_ge(tg_ready, 1)
            now(v.tensor_scalar(ANY[:, :], ANY[:, :], tg(1), None, ALU.mult))
            v.tensor_scalar(MB1[:, :], MI[:, :], 0.0, MASKED, ALU.is_equal, ALU.mult).then_inc(const_copied, 1)
            dve.wait_ge(const_copied, 2)
            prepare(0)
            dve.wait_ge(in_small, SMALL_IN)
            now(v.memset(ROWr[:, :].bitcast(fp32), 0.0))
            now(v.tensor_copy(ROWr[0:1, :], ROW[0:1, :]))
            now(v.tensor_copy(ROWr[32:33, :], ROW[32:33, :]))
            v.tensor_tensor(ROWr[32:33, :], ROW[32:33, :], ROWr[32:33, :].bitcast(fp32), ALU.subtract).then_inc(row_ready, 1)

            for i in range(2):
                dve.wait_ge(a0_s, i + 1)
                now(v.tensor_reduce(MX[:, 4 * i:4 * i + 4], PS[4 + i][:, 0:4 * KC].rearrange("p (b k) -> p b k", b=4), AX.X, ALU.max))
                v.tensor_tensor(SUB[:, i * 4 * KC:(i + 1) * 4 * KC].rearrange("p (b k) -> p b k", b=4),
                                PS[4 + i][:, 0:4 * KC].rearrange("p (b k) -> p b k", b=4),
                                MX[:, 4 * i:4 * i + 4].rearrange("p (b o) -> p b o", o=1).to_broadcast([128, 4, KC]),
                                ALU.subtract).then_inc(a0_sub, 1)
            dve.wait_ge(a0_exp, 2)
            now(v.tensor_reduce(RC[:, 0:B], PB[:, 0:B * KC].rearrange("p (b k) -> p b k", b=B), AX.X, ALU.add))
            now(v.reciprocal(RC[:, 8:8 + B], RC[:, 0:B]))
            now(v.tensor_scalar(RC[:, 0:B], RC[:, 8:8 + B], tg(0), None, ALU.mult))
            for i in range(2):
                dve.wait_ge(a0_o, i + 1)
                for t in range(TH):
                    b = TH * i + t
                    step(v.scalar_tensor_tensor(X[:, b, :], PS[i][:, t * D:(t + 1) * D], RC[:, b:b + 1], X[:, b, :],
                                                ALU.mult, ALU.add))
            settle()
            norm(1, X, XN)
            low_of_xt(1, 0)
            mixture(0, 0)
            summed(0)
            norm(2, X, XN)
            prepare(1)
            attention(0, 1)
            norm(3, X, XN)
            dve.wait_ge(xn_ready, 4 * B)
            norm(4, XN, XM)
            now(v.scalar_tensor_tensor(X[:, :, :].rearrange("p b d -> p (b d)"), XN[:, :, :].rearrange("p b d -> p (b d)"),
                                       tg(5), X[:, :, :].rearrange("p b d -> p (b d)"), ALU.mult, ALU.add))
            low_of_xt(3, 1)
            mixture(1, 1)
            summed(1)
            norm(5, X, XN)
            prepare(3)
            now(v.tensor_reduce(CS[:, :], CT[:, :].rearrange("p (b k) -> p b k", b=B), AX.X, ALU.add))
            v.tensor_scalar(CSB.rearrange("p (b s) -> p b s", b=B),
                            CS[:, :].rearrange("p (b o) -> p b o", o=1).to_broadcast([128, B, S]), 1.0 / KC, None,
                            ALU.mult).then_inc(csb_ready, 1)
            for h in range(2):
                dve.wait_ge(a2_full, h + 1)
                xh = X[:, TH * h:TH * h + TH, :].rearrange("p b d -> p (b d)")
                now(v.scalar_tensor_tensor(xh, PS[4 + h][:, :], tg(2), xh, ALU.mult, ALU.add))
            norm(6, X, XN)
            dve.wait_ge(xn_ready, 7 * B)
            quantise(XN[:, :, :].rearrange("p b d -> p (b d)"), XQ, T).then_inc(xq_ready, 1)
            dve.wait_ge(xq_ready, 1)
            for t in range(B):
                dve.wait_ge(f2_silu, t + 1)
                hg = HG[:, (t % 2) * I2:(t % 2 + 1) * I2]
                v.tensor_tensor(QD[:, 0:I2], hg, PS[2 * (t % 2) + 1][:, 0:I2], ALU.mult).then_inc(f2_used, 1)
                dve.wait_ge(f2_used, t + 1)
                if t >= 2:
                    dve.wait_ge(f2_t, t - 1)
                quantise(QD[:, 0:I2], HQ[:, (t % 2) * I2:(t % 2 + 1) * I2], I2).then_inc(f2_q, 1)
                dve.wait_ge(f2_q, t + 1)
                if t >= 1:
                    dve.wait_ge(f2_down, t)
                    now(v.scalar_tensor_tensor(X[:, t - 1, :], PS[6 + (t - 1) % 2][:, 0:D], tg(6), X[:, t - 1, :],
                                               ALU.mult, ALU.add))
            dve.wait_ge(f2_down, B)
            now(v.scalar_tensor_tensor(X[:, B - 1, :], PS[6 + (B - 1) % 2][:, 0:D], tg(6), X[:, B - 1, :], ALU.mult, ALU.add))
            dve.wait_ge(mask3_in, 16)
            now(v.tensor_scalar(MB3[:, :], MI[:, :], 0.0, MASKED, ALU.is_equal, ALU.mult))
            for m in range(3):
                last = v.tensor_tensor(BD3[:, m, :].rearrange("p (h e) -> p h e", h=NH),
                                       WQK[:, m * DK:(m + 1) * DK].rearrange("p (o e) -> p o e", o=1).to_broadcast([128, NH, DK]),
                                       HM[:, :].rearrange("p (h o) -> p h o", o=1).to_broadcast([128, NH, DK]), ALU.mult)
            last.then_inc(bd3_ready, 1)
            norm(7, X, XN)
            attention(B, 3)
            for h in range(2):
                dve.wait_ge(wo_full, h + 1)
                xh = X[:, TH * h:TH * h + TH, :].rearrange("p b d -> p (b d)")
                now(v.scalar_tensor_tensor(xh, PS[2 + h][:, :], tg(3), xh, ALU.mult, ALU.add))
            norm(8, X, XN)
            low_of_xt(7, 2)
            mixture(2, 3)
            summed(2, last=True)

        @block.tensor
        def _(pe):
            t_ = nc.tensor

            def mm(o, l, r, start=True, stop=True):
                return t_.matmul(o, l, r, start=start, stop=stop)

            def mm3(o, l, r, start, stop):
                mm(o, l[0], r[0], start, False)
                mm(o, l[0], r[1], False, False)
                return mm(o, l[1], r[0], False, stop)

            def turn(k, src, ready):
                for h in range(2):
                    for t in range(TH):
                        i = TH * h + t
                        ready(i)
                        last = t_.transpose(PS[6 + h][:, t * S:(t + 1) * S], src(i), ident[:, :])
                    last.then_inc(xnt_full, 1)

            def normed(n, buf):
                return lambda i: buf[:, i, :], lambda i: pe.wait_ge(xn_ready, n * B + i + 1)

            def logits(n, w, k):
                for t in range(B):
                    if t % TH == 0:
                        pe.wait_ge(xt_ready, 2 * k + t // TH + 1)
                    last = mm(PS[4][:, t * E:(t + 1) * E], XT[:, t * S:(t + 1) * S], w)
                last.then_inc(logit_full, 1)

            def ring(j):
                if j >= NRING:
                    pe.wait_ge(*reader(j - NRING))
                return PS[RING[j % NRING]]

            def mixture(n, layer, first_xtl):
                for s in ORDER[layer]:
                    kind = s["kind"]
                    if kind in ("split", "quantise", "route"):
                        continue
                    e, h, i, j, u = s["e"], s["h"], s["i"], s["job"], s["unit"]
                    x = (XTh[:, h * HALF:(h + 1) * HALF], XTl[:, h * HALF:(h + 1) * HALF])

                    def cols(pair, c0, n, p=128):
                        return tuple(m[0:p, c0:c0 + n] for m in pair)

                    def use(kind):
                        r = area_of(u, kind)
                        if i == 0:
                            pe.wait_ge(lo_done, r["ready"])
                        return r

                    if kind == "gate_up":
                        if i == 0:
                            pe.wait_ge(xtl_ready, first_xtl + 2)
                        xt = cols(x, i * S, S)
                        for m, name in enumerate(("gate", "up")):
                            w = weights(use(name), 0, 2 * I0)
                            mm3(ring(j + m)[:, 0:2 * I0], xt, w, True, True).then_inc(ring_full, 1)
                    elif kind == "turn0":
                        rows = 128 if i < 2 else 2 * I0 - 256
                        if i == 0:
                            pe.wait_ge(dve_freed, max(m["dve"] for m in ORDER[0] if m["kind"] == "gate_up"
                                                      and m["e"] == e and m["h"] == h))
                        o = ring(j)
                        for t in range(TH):
                            at = t * 2 * I0 + i * 128
                            last = t_.transpose(o[0:rows, t * S:(t + 1) * S], SN[:, h, at:at + rows], ident[:, :])
                        last.then_inc(ring_full, 1)
                    elif kind == "down0":
                        if i == 0:
                            use("down")
                            use("down_rest")
                        pe.wait_ge(split_done, hidden_ready(u, h, ("turn0",), i))
                        rows = 128 if i < 2 else 2 * I0 - 256
                        w = weights(area_of(u, "down"), i * D, (i + 1) * D) if i < 2 else weights(area_of(u, "down_rest"), 0, D)
                        first, last = e == 0 and i == 0, e == E0P - 1 and i == 2
                        ins = mm3(PS[4 + h][:, :], w, cols(HID[s["buf"]], i * HALF, HALF, rows), first, last)
                        if last:
                            ins.then_inc(y0_full, 1)
                    elif kind == "up":
                        w = weights(use("up"), i * 128, (i + 1) * 128)
                        pe.wait_ge(xtl_ready, first_xtl + 2)
                        mm3(ring(j)[:, :], w, x, True, True).then_inc(ring_full, 1)
                    elif kind in ("spec1a", "spec2"):
                        width = F2 if kind == "spec1a" else F1
                        r = use("inner")
                        o = ring(j)
                        for f in range(4):
                            if i == 0:
                                pe.wait_ge(split_done, hidden_ready(u, h, ("up",), f))
                            at = f * width + i * 128
                            last = mm3(o[:, :], weights(r, at, at + 128), cols(HID[h], f * HALF, HALF), f == 0, f == 3)
                        last.then_inc(ring_full, 1)
                    elif kind in ("spec0", "spec1b"):
                        r = use("inner")
                        if kind == "spec0":
                            src, buf, nf, at, row = "up", h, 4, 0, e // 4
                        else:
                            src, buf, nf, at, row = "spec1a", 2 + h, 2, 4 * F2, 2 + e // 4
                        if i == 0:
                            pe.wait_ge(row_ready, 1)
                        o = ring(j)
                        mm(o[:, :], onesr[:, :], ROWr[:, row * F1:(row + 1) * F1], True, False)
                        for f in range(nf):
                            if i == 0:
                                pe.wait_ge(split_done, hidden_ready(u, h, (src,), f))
                            last = mm3(o[:, :], cols(HID[buf], f * HALF + i * S, S),
                                       weights(r, at + f * F1, at + (f + 1) * F1), False, f == nf - 1)
                        last.then_inc(ring_full, 1)
                    elif kind == "turn":
                        if i == 0:
                            pe.wait_ge(dve_freed, max(m["dve"] for m in ORDER[1] if m["kind"] in ("spec0", "spec1b")
                                                      and m["e"] == e and m["h"] == h))
                        o = ring(j)
                        for t in range(TH):
                            at = t * F1 + i * 128
                            last = t_.transpose(o[:, t * S:(t + 1) * S], SN[:, h, at:at + 128], ident[:, :])
                        last.then_inc(ring_full, 1)
                    elif kind == "wgt":
                        if h == 0:
                            pe.wait_ge(wgs_ready, n)
                        o = ring(j)
                        for t in range(TH):
                            last = mm(o[0:96, t * S:(t + 1) * S], WGS[:, TH * h + t, :], identb[:, :])
                        last.then_inc(ring_full, 1)
                    elif kind == "spread":
                        if e == 0 and h == 0:
                            pe.wait_ge(act_freed, s["act"] - 1)
                            pe.wait_ge(pool_step, 6)
                        mm(ring(j)[:, :], PICK[:, e:e + 1].to_broadcast([96, 128]),
                           WGT[:, h * HALF:(h + 1) * HALF]).then_inc(ring_full, 1)
                    elif kind == "down":
                        r = use("down")
                        d = s["down"] if i == 3 else s["down"] + 1
                        kinds = ("up",) if layer == 3 or e % 4 == 3 else ("spec2", "turn")
                        pe.wait_ge(split_done, hidden_ready(u, h, kinds, i))
                        if i == 0:
                            if d > 2:
                                pe.wait_ge(down_free, d - 2)
                            if e == 0 and h == 1:
                                pe.wait_ge(wg_ready, n + 1)
                        last = mm3(PS[4 + d % 2][:, :], weights(r, i * D, (i + 1) * D), cols(HID[s["buf"]], i * HALF, HALF),
                                   i == 0, i == 3)
                        if i == 3:
                            last.then_inc(down_full, 1)

            def turn_back(n):
                for b in range(B):
                    if n == 0:
                        pe.wait_ge(y0_copied, b // TH + 1)
                    last = t_.transpose(PS[6 + b // TH][:, (b % TH) * D:(b % TH + 1) * D], XT[:, b * S:(b + 1) * S], ident[:, :])
                    if b % TH == TH - 1:
                        last.then_inc(y_turned, 1)

            def attention(first, mb):
                g0 = first * NG

                def scores(g):
                    b, t = g // NG, g // NG - first
                    if g % NG == 0:
                        pe.wait_ge(bdk_ready, b + 1)
                    if g - g0 >= 3:
                        pe.wait_ge(sub_done, g - 2)
                    o = PS[g % 3][:, 0:GH * KC]
                    c = (g % NG) * GH * KC
                    mm(o, QT[:, t * S:(t + 1) * S], BDK[:, b % 2, c:c + GH * KC], True, False)
                    mask = mb[:, t * KC:(t + 1) * KC].rearrange("p (o k) -> p o k", o=1).to_broadcast([128, GH, KC])
                    mm(o.rearrange("p (h k) -> p h k", h=GH), identb[:, :], mask, False, True).then_inc(s_full, 1)

                def transposes(g):
                    pe.wait_ge(exp_done, g + 1)
                    if g - g0 >= 3:
                        pe.wait_ge(*copied_out(g - 3))
                    for m in range(GH):
                        last = t_.transpose(PS[3 + g % 3][0:KC, m * S:(m + 1) * S],
                                            group(PB, g)[:, m * KC:(m + 1) * KC], ident[:, :])
                    last.then_inc(pt_full, 1)

                def values(g):
                    b, t = g // NG, g // NG - first
                    pe.wait_ge(*copied_out(g))
                    if g % NG == 0 and t >= 2:
                        pe.wait_ge(o_done, b - 1)
                    for m in range(GH):
                        h = (g % NG) * GH + m
                        c = slice(h * (DK + 1), (h + 1) * (DK + 1))
                        at = (g % 3) * HALF + m * S
                        last = mm(PS[6 + b % 2][:, c], PT[:, at:at + S], V1[:, t, c])
                    if g % NG == NG - 1:
                        last.then_inc(o_full, 1)

                for i in range(B * NG + VALUE_LAG):
                    if i < B * NG:
                        scores(g0 + i)
                    if g0 <= g0 + i - TURN_LAG < g0 + B * NG:
                        transposes(g0 + i - TURN_LAG)
                    if i >= VALUE_LAG:
                        values(g0 + i - VALUE_LAG)

            pe.wait_ge(pool_const, 6)
            pe.wait_ge(in_ctx, 16)
            for b in range(B):
                last = t_.transpose(PS[4 + b // 4][:, (b % 4) * KC:(b % 4 + 1) * KC], CTX[:, b, :], ident[0:KC, 0:KC])
                if b % 4 == 3:
                    last.then_inc(ctxt_full, 1)
            turn(0, *normed(0, XN))
            pe.wait_ge(in_small, SMALL_IN)
            for i in range(2):
                pe.wait_ge(xt_ready, i + 1)
                mm(PS[i][0:R0, :], Wu[:, :], XT[:, i * HALF:(i + 1) * HALF]).then_inc(a0_up, 1)
            for i in range(2):
                pe.wait_ge(ct_ready, i + 1)
                mm(PS[2 + i][0:R0, 0:4 * KC], Wv[:, :], CT[:, i * 4 * KC:(i + 1) * 4 * KC]).then_inc(a0_up, 1)
            pe.wait_ge(a0_upc, 4)
            for b in range(B):
                last = mm(PS[4 + b // 4][:, (b % 4) * KC:(b % 4 + 1) * KC], U0T[:, b * S:(b + 1) * S], VP0[:, b * KC:(b + 1) * KC])
                if b % 4 == 3:
                    last.then_inc(a0_s, 1)
            for b in range(B):
                pe.wait_ge(a0_exp, b // 4 + 1)
                last = t_.transpose(PS[6 + b // 4][0:KC, (b % 4) * S:(b % 4 + 1) * S], PB[:, b * KC:(b + 1) * KC], ident[:, :])
                if b % 4 == 3:
                    last.then_inc(a0_pt, 1)
            for b in range(B):
                pe.wait_ge(a0_ptc, b // 4 + 1)
                last = mm(PS[b // 4][:, (b % 4) * D:(b % 4 + 1) * D], PT[:, b * S:(b + 1) * S], CTX[:, b, :])
                if b % 4 == 3:
                    last.then_inc(a0_o, 1)
            turn(1, *normed(1, XN))
            logits(0, GW0[:, :], 1)
            mixture(0, 0, 0)
            pe.wait_ge(split_done, LAST0["hid"])
            turn_back(0)
            turn(2, *normed(2, XN))
            for i in range(2):
                pe.wait_ge(xt_ready, 4 + i + 1)
                mm(PS[i][:, :], WQ1[:, :], XT[:, i * HALF:(i + 1) * HALF]).then_inc(q_full, 1)
            pe.wait_ge(v1_ready, 1)
            pe.wait_ge(q_ready, 2)
            attention(0, MB1)
            turn(3, *normed(4, XM))
            logits(1, RW1[:, :], 3)
            mixture(1, 1, 2)
            pe.wait_ge(y_added, LAST1["add"])
            pe.wait_ge(act_freed, LAST1["act"])
            turn_back(1)
            turn(4, *normed(5, XN))
            pe.wait_ge(csb_ready, 1)
            pe.wait_ge(in_w2, 16 * len(LAYER2))
            for t in range(B):
                if t % TH == 0:
                    pe.wait_ge(xt_ready, 8 + t // TH + 1)
                o = PS[4 + t // TH][:, (t % TH) * D:(t % TH + 1) * D]
                mm(o, XT[:, t * S:(t + 1) * S], W2A[:, 0:D], True, False)
                mm(o, CSB[:, t * S:(t + 1) * S], W2A[:, D:2 * D], False, False)
                last = mm(o, ones[:, :], B2A[:, :], False, True)
                if t % TH == TH - 1:
                    last.then_inc(a2_full, 1)
            pe.wait_ge(wq_ready, 1)
            for m in range(2):
                for c in range(3):
                    k = min(128, I2 - 128 * c)
                    t_.transpose(PS[m][:, c * 128:c * 128 + k], W2R[0:k, m, c, :], ident[0:k, 0:k])
            wd = W2R[:, 2, :, :].rearrange("p c k -> p (c k)")
            for c in range(3):
                k = min(128, I2 - 128 * c)
                last = t_.transpose(PS[2][0:k, c * D:(c + 1) * D], wd[:, c * 128:c * 128 + k], ident[:, :])
            last.then_inc(wq_full, 1)
            turn(5, lambda i: XQ[:, i * D:(i + 1) * D], lambda i: pe.wait_ge(xq_ready, 1))
            pe.wait_ge(wq_copied, 1)

            def down2(t):
                pe.wait_ge(f2_tc, t + 1)
                for c in range(3):
                    k = min(128, I2 - 128 * c)
                    at = 3 * S * (t % 2) + c * S
                    last = mm(PS[6 + t % 2][:, 0:D], HQT[0:k, at:at + S], W2Q[0:k, 2 * I2 + c * D:2 * I2 + (c + 1) * D], c == 0, c == 2)
                last.then_inc(f2_down, 1)

            def up2(t):
                if t % TH == 0:
                    pe.wait_ge(xt_ready, 10 + t // TH + 1)
                if t >= 2:
                    pe.wait_ge(f2_used, t - 1)
                mm(PS[2 * (t % 2)][:, 0:I2], XT[:, t * S:(t + 1) * S], W2Q[:, 0:I2])
                mm(PS[2 * (t % 2) + 1][:, 0:I2], XT[:, t * S:(t + 1) * S], W2Q[:, I2:2 * I2]).then_inc(f2_up, 1)

            up2(0)
            pe.wait_ge(xt_ready, 12)
            for t in range(B):
                if t + 1 < B:
                    up2(t + 1)
                pe.wait_ge(f2_q, t + 1)
                for c in range(3):
                    k = min(128, I2 - 128 * c)
                    last = t_.transpose(PS[4 + t % 2][0:k, c * S:(c + 1) * S],
                                        HQ[:, (t % 2) * I2 + c * 128:(t % 2) * I2 + c * 128 + k], ident[:, :])
                last.then_inc(f2_t, 1)
                down2(t)
            pe.wait_ge(bd3_ready, 1)
            for i in range(2):
                mm(PS[2 + i][:, 0:4 * KC], BD3[:, 1, :], CT[:, i * 4 * KC:(i + 1) * 4 * KC]).then_inc(k3_full, 1)
            for b in range(B):
                last = mm(PS[4 + b // 4][0:KC, (b % 4) * D:(b % 4 + 1) * D], CT[:, b * KC:(b + 1) * KC], BD3[:, 2, :])
                if b % 4 == 3:
                    last.then_inc(v3_full, 1)
            turn(6, *normed(7, XN))
            for i in range(2):
                pe.wait_ge(xt_ready, 12 + i + 1)
                mm(PS[i][:, :], BD3[:, 0, :], XT[:, i * HALF:(i + 1) * HALF]).then_inc(q_full, 1)
            pe.wait_ge(v3_ready, 2)
            pe.wait_ge(q_ready, 4)
            attention(B, MB3)
            pe.wait_ge(o_done, 2 * B)
            for b in range(B):
                last = t_.transpose(PS[b // 4][:, (b % 4) * S:(b % 4 + 1) * S], ON[:, b * D:(b + 1) * D], ident[:, :])
                if b % 4 == 3:
                    last.then_inc(ont_full, 1)
            for b in range(B):
                pe.wait_ge(ont_ready, b // 4 + 1)
                o = PS[2 + b // 4][:, (b % 4) * D:(b % 4 + 1) * D]
                mm(o, ONT[:, b * S:(b + 1) * S], WO3[:, :], True, False)
                last = mm(o, ones[:, :], BO3[:, :], False, True)
                if b % 4 == 3:
                    last.then_inc(wo_full, 1)
            turn(7, *normed(8, XN))
            logits(2, RW3[:, :], 7)
            mixture(2, 3, 4)
            pe.wait_ge(y_added, LAST3["add"])
            pe.wait_ge(act_freed, LAST3["act"])
            turn_back(2)


WEIGH_JOBS = 1
GH = 4
NG = NH // GH
TURN_LAG, EVAC_LAG, VALUE_LAG, WEIGH_LAG = 3, 3, 5, 7


def layouts(x):
    c = np.ascontiguousarray
    cols = lambda m: c(np.moveaxis(m.reshape(m.shape[0], -1, 128), 2, 0).reshape(128, -1))
    own = ["x", "ctx_1024", "mask_Bx1xS2_ik0", "mask_Bx1xSxS2_ik1", "g_xattn", "g_ffn", "L0_xattn_Wu", "L0_xattn_Wv",
           "L0_ffn_wg", "L0_ffn_wu", "L0_ffn_wd", "L0_ffn_swg", "L0_ffn_swu", "L0_ffn_swd",
           "L1_ffn_router_w", "L1_ffn_up_W", "L1_ffn_down_W", "L1_ffn_spec0_W", "L1_ffn_spec1a_W",
           "L1_ffn_spec1b_W", "L1_ffn_spec2_W", "L2_ffn_w_gate", "L2_ffn_w_up", "L2_ffn_w_down",
           "L3_ffn_router_w", "L3_ffn_router_b", "L3_ffn_w1", "L3_ffn_w2"]
    r = {n: c(x[n]) for n in own}
    r["L0_gate_T"] = c(x["L0_ffn_gate_w"].T)
    r["L1_Wq_T"] = c(x["L1_xattn_Wq"].T)
    r["L1_bq_col"] = c(x["L1_xattn_bq"].reshape(128, 1))
    r["L1_ln_g_col"] = c(x["L1_ffn_ln_g"].reshape(128, 1))
    r["L1_ln_b_col"] = c(x["L1_ffn_ln_b"].reshape(128, 1))
    for n in ("up_b", "spec1a_b", "spec2_b", "ln0_g", "ln0_b", "ln1_g", "ln1_b"):
        r[f"L1_{n}_cols"] = cols(x[f"L1_ffn_{n}"])
    r["L1_spec0_b_row"] = c(x["L1_ffn_spec0_b"].reshape(1, -1))
    r["L1_spec1b_b_row"] = c(x["L1_ffn_spec1b_b"].reshape(1, -1))
    w = x["L2_xattn_W"]
    r["L2_W_T"] = c(np.concatenate([w[:, 0:D].T, w[:, D:].T], axis=1))
    r["L2_b_row"] = c(x["L2_xattn_b"].reshape(1, -1))
    r["L3_WqkvT_heads"] = c(np.tile(np.concatenate([x[f"L3_xattn_W{k}"].T for k in "qkv"], axis=1), (NH, 1)))
    r["L3_Wo_T"] = c(x["L3_xattn_Wo"].T)
    r["L3_bo_row"] = c(x["L3_xattn_bo"].reshape(1, -1))
    r["L1_down_b_T"] = c(x["L1_ffn_down_b"].T)
    r["L3_b2_T"] = c(x["L3_ffn_b2"].T)
    r["L3_b1_cols"] = cols(x["L3_ffn_b1"])
    return r


def kernel(**inputs):
    import concourse.bacc as bacc
    from concourse.bass_utils import run_bass_kernel_spmd

    nc = bacc.Bacc("TRN2", target_bir_lowering=False, num_devices=1)
    arrays, handles = {}, {}
    for name, m in layouts({k: np.asarray(v) for k, v in inputs.items()}).items():
        arrays[f"in_{name}"] = m
        handles[name] = nc.dram_tensor(f"in_{name}", m.shape, mybir.dt.from_np(m.dtype), kind="ExternalInput").ap()
    out = nc.dram_tensor("out", (B, S, D), mybir.dt.float32, kind="ExternalOutput").ap()
    program(nc, handles, out)
    r = run_bass_kernel_spmd(nc, [arrays], core_ids=[0])
    return r.results[0]["out"]
```
